# Optimizing a Trainium2 kernel written in Bass

```python
import numpy as np
import jax
import jax.numpy as jnp

def _softmax(x, axis=-1):
    return jax.nn.softmax(x, axis=axis)

def _gelu(x):
    return jax.nn.gelu(x, approximate=True)

def _silu(x):
    return jax.nn.silu(x)

def _sigmoid(x):
    return jax.nn.sigmoid(x)

def _layernorm(x, axis=-1, eps=1e-05):
    m = jnp.mean(x, axis=axis, keepdims=True)
    v = jnp.var(x, axis=axis, keepdims=True)
    return (x - m) / jnp.sqrt(v + eps)

def _scatter_add(tgt, idx, src, axis=0):
    return tgt.at[idx].add(src)

def _segment_sum(src, seg, n):
    return jax.ops.segment_sum(src, seg, n)
kernel_name = 'mk_lm_tower_d1_tok_ids512_r4_755688'

def setup_inputs(seed: int=0):
    np.random.seed(seed)
    _w = jnp.asarray

    def _rec_inputs():
        import jax
        import jax.numpy as jnp
        _rk = jax.random.key(seed)
        x = jax.random.randint(jax.random.fold_in(_rk, 1), (32, 512), 0, 10000, jnp.int32)
        return x
    x = _rec_inputs()

    def _L0_tok_setup():
        import jax, jax.numpy as jnp
        import numpy as np
        B, S, H = (64, 512, 128)
        VOCAB = 10000

        def _syntax_info(token_ids):
            t = token_ids
            opens = (t == 40) | (t == 123) | (t == 91)
            closes = (t == 41) | (t == 125) | (t == 93)
            delta = opens.astype(jnp.int32) - closes.astype(jnp.int32)
            s = jnp.cumsum(delta, axis=1)
            run_min = jax.lax.cummin(s, axis=1)
            nesting = jnp.clip(s - jnp.minimum(run_min, 0), 0, 15)
            segments = jnp.cumsum((t > 39990).astype(jnp.int32), axis=1) % 8
            return (nesting, segments)
        key = jax.random.key(seed)
        k1, k2, k3, k4, k5 = jax.random.split(key, 5)
        token_ids = jax.random.randint(k1, (B, S), 0, VOCAB, dtype=jnp.int64) if jax.config.jax_enable_x64 else jax.random.randint(k1, (B, S), 0, VOCAB, dtype=jnp.int32)
        std = 0.02
        pos_table = jax.random.normal(k2, (S, H), dtype=jnp.float32) * std
        nest_table = jax.random.normal(k3, (16, H), dtype=jnp.float32) * std
        seg_table = jax.random.normal(k4, (8, H), dtype=jnp.float32) * std
        W = jax.random.normal(k5, (3 * H, H), dtype=jnp.float32) * (1.0 / np.sqrt(3 * H))
        return {'token_ids': token_ids, 'pos_table': pos_table, 'nest_table': nest_table, 'seg_table': seg_table, 'W': W}
    _L0_tok_all = _L0_tok_setup()
    _L0_tok_in = {k: v for k, v in _L0_tok_all.items() if k in ('pos_table', 'nest_table', 'seg_table', 'W')}
    del _L0_tok_all

    def _L0_attn_setup():
        import jax, jax.numpy as jnp
        import numpy as np
        N_HEADS = 8
        key = jax.random.key(seed)
        ks = jax.random.split(key, 5)
        b, s, d = (2, 1024, 128)
        return {'x': jax.random.normal(ks[0], (b, s, d), dtype=jnp.float32), 'qkv_w': jax.random.normal(ks[1], (3 * d, d), dtype=jnp.float32) * 0.02, 'qkv_b': jax.random.normal(ks[2], (3 * d,), dtype=jnp.float32) * 0.02, 'out_w': jax.random.normal(ks[3], (d, d), dtype=jnp.float32) * 0.02, 'out_b': jax.random.normal(ks[4], (d,), dtype=jnp.float32) * 0.02}
    _L0_attn_all = _L0_attn_setup()
    _L0_attn_in = {k: v for k, v in _L0_attn_all.items() if k in ('qkv_w', 'qkv_b', 'out_w', 'out_b')}
    del _L0_attn_all

    def _L0_ffn_setup():
        import jax, jax.numpy as jnp
        import numpy as np
        B, T, H = (8, 2048, 128)
        E, R = (4, 16)
        SCALE = 0.04
        key = jax.random.key(seed)
        ks = jax.random.split(key, 7)
        return {'x': jax.random.normal(ks[0], (B, T, H), jnp.float32), 'gate_w': jax.random.normal(ks[1], (E, H), jnp.float32) * SCALE, 'thr_w': jax.random.normal(ks[2], (1, H), jnp.float32) * SCALE, 'fc1_w': jax.random.normal(ks[3], (E, H, H), jnp.float32) * SCALE, 'lora_A': jax.random.normal(ks[4], (E, H, R), jnp.float32) * SCALE, 'lora_B': jax.random.normal(ks[5], (E, R, H), jnp.float32) * SCALE, 'fc2_w': jax.random.normal(ks[6], (E, H, H), jnp.float32) * SCALE}
    _L0_ffn_all = _L0_ffn_setup()
    _L0_ffn_in = {k: v for k, v in _L0_ffn_all.items() if k in ('gate_w', 'thr_w', 'fc1_w', 'lora_A', 'lora_B', 'fc2_w')}
    del _L0_ffn_all
    return {'x': x, 'L0_tok_pos_table': _L0_tok_in['pos_table'], 'L0_tok_nest_table': _L0_tok_in['nest_table'], 'L0_tok_seg_table': _L0_tok_in['seg_table'], 'L0_tok_W': _L0_tok_in['W'], 'L0_attn_qkv_w': _L0_attn_in['qkv_w'], 'L0_attn_qkv_b': _L0_attn_in['qkv_b'], 'L0_attn_out_w': _L0_attn_in['out_w'], 'L0_attn_out_b': _L0_attn_in['out_b'], 'L0_ffn_gate_w': _L0_ffn_in['gate_w'], 'L0_ffn_thr_w': _L0_ffn_in['thr_w'], 'L0_ffn_fc1_w': _L0_ffn_in['fc1_w'], 'L0_ffn_lora_A': _L0_ffn_in['lora_A'], 'L0_ffn_lora_B': _L0_ffn_in['lora_B'], 'L0_ffn_fc2_w': _L0_ffn_in['fc2_w']}

def reference(x, L0_tok_pos_table, L0_tok_nest_table, L0_tok_seg_table, L0_tok_W, L0_attn_qkv_w, L0_attn_qkv_b, L0_attn_out_w, L0_attn_out_b, L0_ffn_gate_w, L0_ffn_thr_w, L0_ffn_fc1_w, L0_ffn_lora_A, L0_ffn_lora_B, L0_ffn_fc2_w):
    import jax
    import jax.numpy as jnp

    def _L0_tok_ref(token_ids, pos_table, nest_table, seg_table, W):
        import jax, jax.numpy as jnp
        import numpy as np
        B, S, H = (64, 512, 128)
        VOCAB = 10000

        def _syntax_info(token_ids):
            t = token_ids
            opens = (t == 40) | (t == 123) | (t == 91)
            closes = (t == 41) | (t == 125) | (t == 93)
            delta = opens.astype(jnp.int32) - closes.astype(jnp.int32)
            s = jnp.cumsum(delta, axis=1)
            run_min = jax.lax.cummin(s, axis=1)
            nesting = jnp.clip(s - jnp.minimum(run_min, 0), 0, 15)
            segments = jnp.cumsum((t > 39990).astype(jnp.int32), axis=1) % 8
            return (nesting, segments)
        b, s = token_ids.shape
        positions = jnp.arange(s)
        pos_emb = jnp.broadcast_to(pos_table[positions][None], (b, s, pos_table.shape[-1]))
        nesting, segments = _syntax_info(token_ids)
        nest_emb = nest_table[nesting]
        seg_emb = seg_table[segments]
        combined = jnp.concatenate([pos_emb, nest_emb, seg_emb], axis=-1)
        return jnp.einsum('bsk,kh->bsh', combined, W)

    def _L0_attn_ref(x, qkv_w, qkv_b, out_w, out_b):
        import jax, jax.numpy as jnp
        import numpy as np
        N_HEADS = 8
        b, s, d = x.shape
        h = N_HEADS
        c = d // h
        factor = 1.0 / jnp.sqrt(jnp.asarray(c, dtype=x.dtype))
        qkv = x @ qkv_w.T + qkv_b
        qkv = qkv.reshape(b, s, h, 3, c)
        q, k, v = (qkv[..., 0, :], qkv[..., 1, :], qkv[..., 2, :])
        scores = jnp.einsum('bshc,bthc->bhst', q, k) * factor
        attn = jax.nn.softmax(scores, axis=-1)
        ctx = jnp.einsum('bhst,bthc->bshc', attn, v).reshape(b, s, d)
        return ctx @ out_w.T + out_b

    def _L0_ffn_ref(x, gate_w, thr_w, fc1_w, lora_A, lora_B, fc2_w):
        import jax, jax.numpy as jnp
        import numpy as np
        B, T, H = (8, 2048, 128)
        E, R = (4, 16)
        SCALE = 0.04
        b, t, h = x.shape
        e = gate_w.shape[0]
        xf = x.reshape(-1, h)
        gate_logits = jax.nn.softmax(xf @ gate_w.T, axis=-1)
        thresholds = jax.nn.sigmoid(xf @ thr_w.T) * (1.0 / e)
        adapted = gate_logits - thresholds
        selected = (adapted >= 0).astype(xf.dtype)
        weights = adapted * selected
        wsum = jnp.sum(weights, axis=-1, keepdims=True)
        wsum = jnp.where(wsum == 0, jnp.ones_like(wsum), wsum)
        weights = weights / wsum
        hidden = jax.nn.relu(jnp.einsum('ni,ehi->neh', xf, fc1_w))
        lo = jnp.einsum('neh,ehr->ner', hidden, lora_A)
        lo = jnp.einsum('ner,ero->neo', lo, lora_B)
        expert_out = jnp.einsum('neo,edo->ned', lo, fc2_w)
        out = jnp.einsum('ne,ned->nd', weights, expert_out)
        return out.reshape(b, t, h)
    h = _L0_tok_ref(x, L0_tok_pos_table, L0_tok_nest_table, L0_tok_seg_table, L0_tok_W)
    h = h + _L0_attn_ref(_layernorm(h, axis=-1), L0_attn_qkv_w, L0_attn_qkv_b, L0_attn_out_w, L0_attn_out_b)
    h = h + _L0_ffn_ref(_layernorm(h, axis=-1), L0_ffn_gate_w, L0_ffn_thr_w, L0_ffn_fc1_w, L0_ffn_lora_A, L0_ffn_lora_B, L0_ffn_fc2_w)
    return h

_drawn_inputs = setup_inputs


def setup_inputs(seed=0):
    import zlib

    import numpy as np

    out = dict(_drawn_inputs(seed))
    spreads = {}
    factors = {'L0_ffn_thr_w': 75.997}
    for name, (base, spread) in spreads.items():
        noise = np.random.default_rng([zlib.crc32(name.encode()), seed]).standard_normal(out[name].shape)
        drawn = base * np.exp(spread * noise) if base else spread * noise
        out[name] = jnp.asarray(drawn.astype(out[name].dtype))
    for name, factor in factors.items():
        out[name] = (out[name] * factor).astype(out[name].dtype)
    return out
```

```python
from contextlib import ExitStack

import concourse.bass as bass
from concourse import mybir

ALU = mybir.AluOpType
ACT = mybir.ActivationFunctionType
AX = mybir.AxisListType
F32 = mybir.dt.float32
BF16 = mybir.dt.bfloat16
I32 = mybir.dt.int32

P = 128
NSEQ, S = 32, 512
NT = S // P
NH, HC = 8, 16
NE, NR = 4, 16
Q = 32
NNEST, NSEG = 16, 8
SEGROW = 64
HOT = 96
STK = 6 * HC
KROWS = STK + 3 * NH
SLOTS = 16
U = 4
EPS = 1e-5
QSCALE = HC ** -0.5
Q_READS = [(0, 0, 3), (3 * HC, 0, 2), (5 * HC, 0, 1)]
K_READS = [(0, 0, 3), (3 * HC, 1, 2), (5 * HC, 2, 1)]


def tower(nc, x, posT, catT, consts, ident, tokW, qkvT, qkb, bv, ob, woT, wo_q, gateT, fc1T, loA, loBT, fc2T, out):
    ids_dram = nc.dram_tensor("ids_dram", (NSEQ, 2, S), BF16, kind="Internal").ap()
    stack_dram = nc.dram_tensor("stack_dram", (2, 3, HC, NH, S), BF16, kind="Internal").ap()
    den_dram = nc.dram_tensor("den_dram", (NH, S), F32, kind="Internal").ap()
    rden_dram = nc.dram_tensor("rden_dram", (NH, S), F32, kind="Internal").ap()

    with ExitStack() as ctx:
        def sb(name, shape, dt=F32):
            return ctx.enter_context(nc.sbuf_tensor(name, shape, dt))

        def sem(name):
            return ctx.enter_context(nc.semaphore(name))

        sc = ctx.enter_context(nc.psum_tensor("sc", [P, 2, 2, S], F32))
        pv = ctx.enter_context(nc.psum_tensor("pv", [P, S], F32))
        mx = ctx.enter_context(nc.psum_tensor("mx", [P, 2, S], F32))
        aux = ctx.enter_context(nc.psum_tensor("aux", [P, S], F32))
        aux_tiles = aux[:].rearrange("p (j n) -> p j n", j=NT)

        probs = sb("probs", [P, 8, 2, S])
        posT_sb = probs[:, 6, 0, :]
        fc2T_sb = probs[:, 6, 1, :].rearrange("p (e n) -> p e n", e=NE)
        catT_sb = sb("catT_sb", [P, HOT])
        const_sb = sb("const_sb", [P, 4 + NH])
        id32 = sb("id32", [P, P])
        id16 = sb("id16", [P, P], BF16)
        tokW_sb = sb("tokW_sb", [P, 3, P])
        qkvT_sb = sb("qkvT_sb", [P, 3, P])
        qkb_sb = sb("qkb_sb", [P, 2])
        qb_sb = sb("qb_sb", [P, 1])
        bv_sb = sb("bv_sb", [P, 1])
        ob_sb = sb("ob_sb", [1, P])
        ones_sb = sb("ones_sb", [1, P])
        woT_sb = sb("woT_sb", [P, P])
        wo_q_sb = sb("wo_q_sb", [P, 2, P])
        gateT_sb = sb("gateT_sb", [P, Q])
        fc1T_sb = sb("fc1T_sb", [P, NE, P])
        loA_sb = sb("loA_sb", [P, NE, Q])
        loBT_sb = sb("loBT_sb", [P, NE, Q])
        exp_w = sb("exp_w", [P, P])
        posW = sb("posW", [P, NT, P])
        obias = sb("obias", [P, P])
        table = sb("table", [HOT, P], BF16)
        minus_half = sb("minus_half", [P, NT])
        eps_sb = sb("eps_sb", [P, NT])
        after = sb("after", [P, 1])

        xf, opens, closes, zeros, delta, depth, lowest = (probs[0:NSEQ, i // 2, i % 2, :] for i in range(7))
        xi, segi = (probs[0:NSEQ, 4, i, :].bitcast(I32) for i in range(2))
        ids_sb = sb("ids_sb", [NSEQ, 2, S], BF16)
        tab = sb("tab", [HOT, 4, P])
        tab16 = sb("tab16", [HOT, 2, P], BF16)

        ids_b = sb("ids_b", [HOT, S], BF16)
        onehot = sb("onehot", [HOT, S], BF16)
        h_sb = sb("h_sb", [P, NT, P])
        hb_sb = sb("hb_sb", [P, U, NT, P])
        bn1 = sb("bn1", [P, NT, 6])
        mv1 = sb("mv1", [P, NT, 2])
        ve1 = sb("ve1", [P, NT])
        rstd1 = sb("rstd1", [P, NT])
        xn = sb("xn", [P, NT, P])
        xnT = sb("xnT", [P, S])
        qk32 = sb("qk32", [P, 2, S])
        qkr = sb("qkr", [P, 2, S])
        pieces = sb("pieces", [P, 2, 3, S], BF16)
        vals = sb("vals", [P, U, NT, NH, Q])
        qstk = sb("qstk", [P, U, NH, S], BF16)
        kstk = sb("kstk", [P, U, NH, S], BF16)
        negmax = sb("negmax", [P, NH, NT])
        mres = sb("mres", [P, NT, NH])
        mpc = sb("mpc", [P, NT, 3, NH], BF16)
        mT = sb("mT", [3 * NH, S], BF16)
        ctx_sb = sb("ctx_sb", [P, 2, 2, S])
        den = sb("den", [P, Q])
        rden = sb("rden", [P, Q])
        rdenb = sb("rdenb", [P, 2, S])
        ctxn = sb("ctxn", [P, 2, S])
        h2 = sb("h2", [P, U, NT, P])
        bn2 = sb("bn2", [P, NT, 6])
        mv2 = sb("mv2", [P, NT, 2])
        ve2 = sb("ve2", [P, NT])
        rstd2 = sb("rstd2", [P, NT])
        xn2 = sb("xn2", [P, NT, P])
        xn2T = sb("xn2T", [P, S])
        gat = sb("gat", [P, P])
        logit = sb("logit", [P, NT, 5])
        lmax = sb("lmax", [P, NT])
        lsub = sb("lsub", [P, NT, 5])
        lexp = sb("lexp", [P, NT, 5])
        gden = sb("gden", [P, NT, 2])
        grec = sb("grec", [P, NT, 2])
        gsm = sb("gsm", [P, NT, NE])
        gad = sb("gad", [P, NT, NE])
        gsel = sb("gsel", [P, NT, NE])
        wsum = sb("wsum", [P, NT])
        wsafe = sb("wsafe", [P, NT])
        wrec = sb("wrec", [P, NT])
        wts = sb("wts", [P, NT, NE])
        wrow = sb("wrow", [P, NT, NE, Q])
        hid = sb("hid", [P, NE, S])
        lo_sb = sb("lo_sb", [P, S])
        low = sb("low", [P, S])
        out_sb = sb("out_sb", [P, NT, P])

        s_x = sem("s_x")
        s_w = sem("s_w")
        s_set = sem("s_set")
        s_setmm = sem("s_setmm")
        s_setcp = sem("s_setcp")
        s_idset = sem("s_idset")
        s_qb = sem("s_qb")
        s_table = sem("s_table")
        s_idsout = sem("s_idsout")
        s_const = sem("s_const")
        s_pconst = sem("s_pconst")
        s_ids = sem("s_ids")
        s_hot = sem("s_hot")
        s_embmm, s_h, s_hb = sem("s_embmm"), sem("s_h"), sem("s_hb")
        s_bn1, s_mv1, s_ve1, s_rstd1, s_xn = sem("s_bn1"), sem("s_mv1"), sem("s_ve1"), sem("s_rstd1"), sem("s_xn")
        s_xnTmm, s_xnT = sem("s_xnTmm"), sem("s_xnT")
        s_qmm, s_kmm, s_vmm = sem("s_qmm"), sem("s_kmm"), sem("s_vmm")
        s_qk32 = sem("s_qk32")
        s_v = sem("s_v")
        s_pc0, s_res0, s_pc1, s_pc2 = sem("s_pc0"), sem("s_res0"), sem("s_pc1"), sem("s_pc2")
        s_pcout = sem("s_pcout")
        s_stk = sem("s_stk")
        s_mxmm, s_max = sem("s_mxmm"), sem("s_max")
        s_mp = sem("s_mp")
        s_mTmm, s_mT, s_mrow = sem("s_mTmm"), sem("s_mT"), sem("s_mrow")
        s_score, s_exp, s_pv, s_ctx = sem("s_score"), sem("s_exp"), sem("s_pv"), sem("s_ctx")
        s_denout, s_denin, s_rden, s_rdout = sem("s_denout"), sem("s_denin"), sem("s_rden"), sem("s_rdout")
        s_rdin = [sem(f"s_rdin{g}") for g in range(2)]
        s_ctxn = sem("s_ctxn")
        s_projmm, s_h2 = sem("s_projmm"), sem("s_h2")
        s_bn2, s_mv2, s_ve2, s_rstd2, s_xn2 = sem("s_bn2"), sem("s_mv2"), sem("s_ve2"), sem("s_rstd2"), sem("s_xn2")
        s_xn2Tmm, s_xn2T = sem("s_xn2Tmm"), sem("s_xn2T")
        s_gatmm, s_gat, s_gatTmm, s_logit = sem("s_gatmm"), sem("s_gat"), sem("s_gatTmm"), sem("s_logit")
        s_gate = sem("s_gate")
        s_gexp, s_wrow = sem("s_gexp"), sem("s_wrow")
        s_fc1mm, s_hid = sem("s_fc1mm"), sem("s_hid")
        s_lomm, s_lo, s_wTmm, s_low = sem("s_lomm"), sem("s_lo"), sem("s_wTmm"), sem("s_low")
        s_outmm, s_out, s_store = sem("s_outmm"), sem("s_out"), sem("s_store")

        def upto(eng, s, b, per=1, k=None):
            k = per if k is None else k
            if isinstance(b, int):
                value = min(per * b + k, per * NSEQ)
                if value > 0:
                    eng.wait_ge(s, value)
            else:
                eng.wait_ge(s, b * per + k)

        def runs(b):
            return not isinstance(b, int) or 0 <= b < NSEQ

        def steps(eng, step):
            first = 3
            rounds = (NSEQ - 3 - first) // U
            for t in range(-2, first):
                step(t, t % U)
            with eng.Fori(0, rounds) as i:
                for u in range(U):
                    step(i * U + (first + u), (first + u) % U)
            for t in range(first + rounds * U, NSEQ + 2):
                step(t, t % U)

        block = ctx.enter_context(nc.Block())

        @block.sync
        def _(sp):
            sp.dma_start(xi, x).then_inc(s_x, 16)
            for dst, src in [(const_sb[:], consts), (id32[:], ident), (catT_sb[:], catT),
                             (tokW_sb[:], tokW), (posT_sb, posT), (qkvT_sb[:], qkvT), (qkb_sb[:], qkb),
                             (bv_sb[:], bv), (ob_sb[:], ob), (woT_sb[:], woT), (wo_q_sb[:], wo_q),
                             (gateT_sb[:], gateT), (fc1T_sb[:], fc1T), (loA_sb[:], loA), (loBT_sb[:], loBT),
                             (fc2T_sb, fc2T)]:
                sp.dma_start(dst, src).then_inc(s_w, 16)
            sp.wait_ge(s_idset, 2)
            sp.dma_start(ids_dram, ids_sb[:]).then_inc(s_idsout, 16)
            sp.wait_ge(s_idsout, 16)

            def load_ids(b):
                upto(sp, s_hot, b - 1)
                sp.dma_start(ids_b[0:SEGROW, :], ids_dram[b, 0].partition_broadcast(SEGROW)).then_inc(s_ids, 16)
                sp.dma_start(ids_b[SEGROW:HOT, :], ids_dram[b, 1].partition_broadcast(HOT - SEGROW)).then_inc(s_ids, 16)

            def store_pieces(b, side):
                for p, ready in ((0, s_pc0), (1, s_pc1), (2, s_pc2)):
                    upto(sp, ready, b, 2, side + 1)
                    if p == 0:
                        upto(sp, s_stk, b - 1, 96)
                    sp.dma_start(stack_dram[side, p].rearrange("c h s -> h c s"),
                                 pieces[:, side, p, :]).then_inc(s_pcout, 16)

            def load_stacks(b, u):
                upto(sp, s_pcout, b, 96)
                upto(sp, s_score, b - U, SLOTS)
                for row, p, n in Q_READS:
                    sp.dma_start(qstk[row:row + n * HC, u, :, :],
                                 stack_dram[0, p:p + n].rearrange("p c h s -> (p c) h s")).then_inc(s_stk, 16)
                for row, p, n in K_READS:
                    sp.dma_start(kstk[row:row + n * HC, u, :, :],
                                 stack_dram[1, p].unsqueeze(0).broadcast_to([n, HC, NH, S])).then_inc(s_stk, 16)

            def load_max(b, u):
                upto(sp, s_mT, b)
                sp.dma_start(qstk[STK:KROWS, u, :, :],
                             mT[:].unsqueeze(1).broadcast_to([3 * NH, NH, S])).then_inc(s_mrow, 16)

            def store_den(b, g, u):
                upto(sp, s_ctx, b, 2, g + 1)
                upto(sp, s_denin, b - 1, 16)
                sp.dma_start(den_dram[4 * g:4 * g + 4], ctx_sb[HC:P:Q, u % 2, g, :]).then_inc(s_denout, 16)

            def load_den(b):
                upto(sp, s_denout, b, 32)
                upto(sp, s_rden, b - 1)
                sp.dma_start(den[:], den_dram.rearrange("h (k s) -> (h k) s", s=Q)).then_inc(s_denin, 16)

            def store_rden(b):
                upto(sp, s_rden, b)
                for g in range(2):
                    upto(sp, s_rdin[g], b - 1, 16)
                sp.dma_start(rden_dram.rearrange("h (k s) -> (h k) s", s=Q), rden[:]).then_inc(s_rdout, 16)

            def load_rden(b):
                for g in range(2):
                    upto(sp, s_ctxn, b - 1, 2, g + 1)
                    if g == 0:
                        upto(sp, s_rdout, b, 16)
                    sp.dma_start(rdenb[:, g, :], rden_dram[4 * g:4 * g + 4].unsqueeze(1).broadcast_to([4, Q, S])
                                 ).then_inc(s_rdin[g], 16)

            def store_out(b):
                upto(sp, s_out, b)
                sp.dma_start(out[b].rearrange("(j p) d -> p j d", p=P), out_sb[:]).then_inc(s_store, 16)

            def step(t, u):
                if runs(t - 1):
                    store_den(t - 1, 1, (u - 1) % U)
                    load_den(t - 1)
                    store_rden(t - 1)
                    load_rden(t - 1)
                if runs(t + 2):
                    store_pieces(t + 2, 0)
                    store_pieces(t + 2, 1)
                if runs(t):
                    store_den(t, 0, u)
                if runs(t + 2):
                    load_stacks(t + 2, (u + 2) % U)
                if runs(t + 3):
                    load_ids(t + 3)
                if runs(t - 2):
                    store_out(t - 2)
                if runs(t + 1):
                    load_max(t + 1, (u + 1) % U)

            load_ids(0)
            steps(sp, step)
            sp.wait_ge(s_store, 16 * NSEQ)

        @block.gpsimd
        def _(pool):
            pool.wait_ge(s_w, 16 * 16)
            pool.memset(vals[:, :, :, :, HC:Q], 1.0).then_inc(s_pconst, 1)

            def rstd(b, mv, ve, rs, s_mv, s_ve, s_rs, s_used):
                upto(pool, s_mv, b, NT)
                upto(pool, s_used, b - 1, NT)
                pool.tensor_tensor(ve[:], mv[:, :, 1], eps_sb[:], ALU.add).then_inc(s_ve, 1)
                upto(pool, s_ve, b)
                pool.tensor_tensor(rs[:], ve[:], minus_half[:], ALU.pow).then_inc(s_rs, 1)

            def add_bias(b, u):
                upto(pool, s_h, b)
                upto(pool, s_h2, b - U)
                pool.tensor_tensor(hb_sb[:, u], h_sb[:], obias[:].unsqueeze(1).broadcast_to([P, NT, P]),
                                   ALU.add).then_inc(s_hb, 1)

            def residual(b, side):
                upto(pool, s_pc0, b, 2, side + 1)
                pool.tensor_tensor(qkr[:, side, :], qk32[:, side, :], pieces[:, side, 0, :],
                                   ALU.subtract).then_inc(s_res0, 1)

            def third(b, side):
                upto(pool, s_pc1, b, 2, side + 1)
                upto(pool, s_pcout, b - 1, 96)
                pool.tensor_tensor(pieces[:, side, 2, :], qkr[:, side, :], pieces[:, side, 1, :],
                                   ALU.subtract).then_inc(s_pc2, 1)

            def normalise(b, g, u):
                upto(pool, s_rdin[g], b, 16)
                upto(pool, s_projmm, b - 1)
                pool.tensor_tensor(ctxn[:, g, :], ctx_sb[:, u % 2, g, :], rdenb[:, g, :],
                                   ALU.mult).then_inc(s_ctxn, 1)

            pool.wait_ge(s_setcp, 4)
            pool.wait_ge(s_const, 3)

            def step(t, u):
                if runs(t + 2):
                    rstd(t + 2, mv1, ve1, rstd1, s_mv1, s_ve1, s_rstd1, s_xn)
                    add_bias(t + 2, (u + 2) % U)
                    for side in range(2):
                        residual(t + 2, side)
                        third(t + 2, side)
                if runs(t - 1):
                    for g in range(2):
                        normalise(t - 1, g, (u - 1) % U)
                    rstd(t - 1, mv2, ve2, rstd2, s_mv2, s_ve2, s_rstd2, s_xn2)

            steps(pool, step)

        @block.scalar
        def _(act):
            act.wait_ge(s_w, 16 * 16)
            act.mul(qb_sb[:], qkb_sb[:, 0:1], QSCALE).then_inc(s_qb, 1)
            act.wait_ge(s_qb, 1)

            def exp(b, c):
                upto(act, s_score, b, SLOTS, c + 1)
                upto(act, s_pv, b, 8, 2 * (c // 4) - 2)
                act.activation(probs[:, c % 8], sc[:, c % 2], ACT.Exp).then_inc(s_exp, 1)

            def copy_xnT(b):
                upto(act, s_xnTmm, b)
                upto(act, s_vmm, b - 1)
                act.copy(xnT[:], aux[:]).then_inc(s_xnT, 1)

            def copy_qk(b, side):
                upto(act, (s_qmm, s_kmm)[side], b)
                upto(act, s_res0, b - 1, 2, side + 1)
                act.activation(qk32[:, side, :], aux[:], ACT.Identity,
                               bias=(qb_sb[:], qkb_sb[:, 1:2])[side], scale=(QSCALE, 1.0)[side]).then_inc(s_qk32, 1)
                upto(act, s_qk32, b, 2, side + 1)
                upto(act, s_pcout, b - 1, 96)
                act.copy(pieces[:, side, 0, :], qk32[:, side, :]).then_inc(s_pc0, 1)

            def copy_v(b, u):
                upto(act, s_vmm, b)
                upto(act, s_pv, b - U, 8)
                act.copy(vals[:, u, :, :, 0:HC], aux[:].rearrange("p (j h c) -> p j h c", j=NT, h=NH)).then_inc(s_v, 1)

            def copy_mT(b):
                upto(act, s_mTmm, b)
                upto(act, s_mrow, b - 1, 16)
                act.copy(mT[:], aux[0:3 * NH, :]).then_inc(s_mT, 1)

            def copy_ctx(b, g, u):
                upto(act, s_pv, b, 8, 4 * g + 4)
                upto(act, s_ctxn, b - 2, 2, g + 1)
                upto(act, s_denout, b - 2, 32)
                act.copy(ctx_sb[:, u % 2, g, :], pv[:]).then_inc(s_ctx, 1)

            def copy_xn2T(b):
                upto(act, s_xn2Tmm, b)
                upto(act, s_fc1mm, b - 1, NE)
                act.copy(xn2T[:], aux[:]).then_inc(s_xn2T, 1)

            def copy_gat(b):
                upto(act, s_gatmm, b)
                upto(act, s_gatTmm, b - 1)
                act.copy(gat[:], aux[:, 0:P]).then_inc(s_gat, 1)

            def gate_exp(b):
                upto(act, s_gate, b, 13, 3)
                upto(act, s_gate, b - 1, 13, 7)
                act.activation(lexp[:], lsub[:], ACT.Exp).then_inc(s_gexp, 1)

            def spread_weights(b):
                upto(act, s_gate, b, 13)
                upto(act, s_wTmm, b - 1)
                act.copy(wrow[:], wts[:].unsqueeze(3).broadcast_to([P, NT, NE, Q])).then_inc(s_wrow, 1)

            def relu(b, e):
                upto(act, s_fc1mm, b, NE, e + 1)
                upto(act, s_lomm, b - 1)
                act.activation(hid[:, e, :], aux[:], ACT.Relu).then_inc(s_hid, 1)

            def copy_lo(b):
                upto(act, s_lomm, b)
                upto(act, s_low, b - 1)
                act.copy(lo_sb[:], aux[:]).then_inc(s_lo, 1)

            def step(t, u):
                for c in range(SLOTS):
                    if runs(t):
                        exp(t, c)
                    if c == 2 and runs(t + 2):
                        copy_xnT(t + 2)
                    if c == 2 and runs(t - 2):
                        gate_exp(t - 2)
                    if c in (3, 4) and runs(t + 2):
                        copy_qk(t + 2, c - 3)
                    if c == 3 and runs(t - 1):
                        copy_ctx(t - 1, 1, (u - 1) % U)
                    if c == 5 and runs(t + 2):
                        copy_v(t + 2, (u + 2) % U)
                    if c in (6, 7, 8) and runs(t - 2):
                        relu(t - 2, c - 5)
                    if c == 8 and runs(t - 2):
                        spread_weights(t - 2)
                    if c == 9 and runs(t - 2):
                        copy_lo(t - 2)
                    if c == 11 and runs(t):
                        copy_ctx(t, 0, u)
                    if c == 12 and runs(t + 1):
                        copy_mT(t + 1)
                    if c == 13 and runs(t - 1):
                        copy_xn2T(t - 1)
                    if c == 14 and runs(t - 1):
                        copy_gat(t - 1)
                    if c == 15 and runs(t - 1):
                        relu(t - 1, 0)

            steps(act, step)

        @block.tensor
        def _(pe):
            pe.wait_ge(s_w, 16 * 16)
            pe.wait_ge(s_const, 2)

            for j in range(NT):
                mm = pe.matmul(aux_tiles[:, j, :], posT_sb[:, j * P:(j + 1) * P], tokW_sb[:, 0, :], start=True, stop=True)
            mm.then_inc(s_setmm, 1)
            pe.matmul(mx[0:SEGROW, 0, 0:P], catT_sb[:, 0:SEGROW], tokW_sb[:, 1, :], start=True, stop=True)
            pe.matmul(mx[SEGROW:HOT, 0, 0:P], catT_sb[:, SEGROW:HOT], tokW_sb[:, 2, :], start=True, stop=True).then_inc(s_setmm, 1)
            for e in range(NE):
                mm = pe.matmul(mx[Q * e:Q * e + Q, 1, 0:P], loBT_sb[:, e, :], fc2T_sb[:, e, :], start=True, stop=True)
            mm.then_inc(s_setmm, 1)
            pe.matmul(pv[:, 0:P], bv_sb[:].broadcast_to([P, P]), woT_sb[:], start=True, stop=False)
            pe.matmul(pv[:, 0:P], ones_sb[:], ob_sb[:], start=False, stop=True).then_inc(s_setmm, 1)
            pe.wait_ge(s_setcp, 4)
            pe.wait_ge(s_table, 1)
            pe.wait_ge(s_pconst, 1)
            pe.wait_ge(s_const, 3 + U)

            def scores_T(b, c, u):
                g, half, h = c // 8, c // 4 % 2, c // 8 * 4 + c % 4
                if c == 0:
                    upto(pe, s_mrow, b, 16)
                upto(pe, s_exp, b, SLOTS, c - 1)
                for jj in range(2):
                    j = 2 * half + jj
                    mm = pe.matmul(sc[:, c % 2, jj, :], kstk[0:KROWS, u, h, j * P:(j + 1) * P],
                                   qstk[0:KROWS, u, h, :], start=True, stop=True)
                mm.then_inc(s_score, 1)

            def values(b, r, jj, u):
                g, half = r // 2, r % 2
                if jj == 0:
                    upto(pe, s_exp, b, SLOTS, 4 * r + 4)
                    if half == 0:
                        upto(pe, s_ctx, b, 2, g)
                for i in range(4):
                    mm = pe.matmul(pv[Q * i:Q * i + Q, :], vals[:, u, 2 * half + jj, 4 * g + i, :],
                                   probs[:, 4 * (r % 2) + i, jj, :],
                                   start=(half == 0 and jj == 0), stop=(half == 1 and jj == 1))
                mm.then_inc(s_pv, 1)

            def scores(b, m, u):
                h, j = m // NT, m % NT
                if m == 0:
                    upto(pe, s_stk, b, 96)
                upto(pe, s_max, b, 32, m - 1)
                pe.matmul(mx[:, m % 2, :], qstk[0:STK, u, h, j * P:(j + 1) * P],
                          kstk[0:STK, u, h, :], start=True, stop=True).then_inc(s_mxmm, 1)

            def embed(b):
                upto(pe, s_hot, b)
                for j in range(NT):
                    mm = pe.matmul(aux_tiles[:, j, :], onehot[:, j * P:(j + 1) * P], table[:], start=True, stop=True)
                mm.then_inc(s_embmm, 1)

            def turn(b, src, ready, signal):
                upto(pe, ready, b, NT)
                for j in range(NT):
                    mm = pe.transpose(aux_tiles[:, j, :], src[:, j, :], id32[:])
                mm.then_inc(signal, 1)

            def qk(b, side):
                upto(pe, s_xnT, b)
                pe.matmul(aux[:], qkvT_sb[:, side, :], xnT[:], start=True, stop=True).then_inc((s_qmm, s_kmm)[side], 1)

            def v(b):
                for j in range(NT):
                    mm = pe.matmul(aux_tiles[:, j, :], xnT[:, j * P:(j + 1) * P], qkvT_sb[:, 2, :], start=True, stop=True)
                mm.then_inc(s_vmm, 1)

            def turn_max(b):
                upto(pe, s_mp, b, 4)
                for j in range(NT):
                    mm = pe.matmul(aux[0:3 * NH, j * P:(j + 1) * P], mpc[:, j].rearrange("p a h -> p (a h)"), id16[:],
                                   start=True, stop=True)
                mm.then_inc(s_mTmm, 1)

            def project(b):
                upto(pe, s_ctxn, b, 2)
                for j in range(NT):
                    for g in range(2):
                        mm = pe.matmul(aux_tiles[:, j, :], ctxn[:, g, j * P:(j + 1) * P], wo_q_sb[:, g, :],
                                       start=(g == 0), stop=(g == 1))
                mm.then_inc(s_projmm, 1)

            def gates(b):
                upto(pe, s_xn2T, b)
                for j in range(NT):
                    mm = pe.matmul(aux[Q * j:Q * j + Q, 0:P], gateT_sb[:], xn2T[:, j * P:(j + 1) * P], start=True, stop=True)
                mm.then_inc(s_gatmm, 1)

            def turn_gates(b):
                upto(pe, s_gat, b)
                pe.transpose(aux[:, 0:P], gat[:], id32[:]).then_inc(s_gatTmm, 1)

            def fc1(b, e):
                pe.matmul(aux[:], fc1T_sb[:, e, :], xn2T[:], start=True, stop=True).then_inc(s_fc1mm, 1)

            def low_rank(b):
                upto(pe, s_hid, b, NE)
                for e in range(NE):
                    mm = pe.matmul(aux[Q * e:Q * e + Q, :], loA_sb[:, e, :], hid[:, e, :], start=True, stop=True)
                mm.then_inc(s_lomm, 1)

            def turn_weights(b):
                upto(pe, s_wrow, b)
                for j in range(NT):
                    mm = pe.transpose(aux_tiles[:, j, :], wrow[:, j].rearrange("p e q -> p (e q)"), id32[:])
                mm.then_inc(s_wTmm, 1)

            def experts_out(b):
                upto(pe, s_low, b)
                for j in range(NT):
                    mm = pe.matmul(aux_tiles[:, j, :], low[:, j * P:(j + 1) * P], exp_w[:], start=True, stop=True)
                mm.then_inc(s_outmm, 1)

            def step(t, u):
                def aux_task(c):
                    if c == 0 and runs(t + 2):
                        upto(pe, s_hid, t - 2, NE, 1)
                        upto(pe, s_mT, t)
                        upto(pe, s_v, t + 1)
                        embed(t + 2)
                    if c == 1 and runs(t - 2):
                        upto(pe, s_h, t + 2)
                        upto(pe, s_hid, t - 2, NE, 1)
                        turn_gates(t - 2)
                    if c == 2 and runs(t + 2):
                        upto(pe, s_logit, t - 2)
                        turn(t + 2, xn, s_xn, s_xnTmm)
                    if c == 3 and runs(t + 2):
                        qk(t + 2, 0)
                    if c == 4 and runs(t + 2):
                        upto(pe, s_qk32, t + 2, 2, 1)
                        qk(t + 2, 1)
                    if c == 5 and runs(t + 2):
                        upto(pe, s_qk32, t + 2, 2)
                        v(t + 2)
                    if c == 6 and runs(t - 2):
                        upto(pe, s_v, t + 2)
                        upto(pe, s_logit, t - 2)
                        fc1(t - 2, 1)
                    if c in (7, 8) and runs(t - 2):
                        upto(pe, s_hid, t - 2, NE, c - 5)
                        fc1(t - 2, c - 5)
                    if c == 9 and runs(t - 2):
                        low_rank(t - 2)
                    if c == 10 and runs(t - 2):
                        upto(pe, s_lo, t - 2)
                        turn_weights(t - 2)
                    if c == 11 and runs(t - 1):
                        upto(pe, s_v, t + 2)
                        upto(pe, s_low, t - 2)
                        project(t - 1)
                    if c == 12 and runs(t + 1):
                        upto(pe, s_v, t + 2)
                        upto(pe, s_h2, t - 1)
                        turn_max(t + 1)
                    if c == 13 and runs(t - 1):
                        upto(pe, s_mT, t + 1)
                        upto(pe, s_out, t - 2)
                        turn(t - 1, xn2, s_xn2, s_xn2Tmm)
                    if c == 14 and runs(t - 1):
                        gates(t - 1)
                    if c == 15 and runs(t - 1):
                        upto(pe, s_gat, t - 1)
                        fc1(t - 1, 0)

                for c in range(SLOTS):
                    if runs(t):
                        scores_T(t, c, u)
                    mine = [m for m in range(3 * c, min(3 * c + 3, 32))] if runs(t + 1) else []
                    for m in mine[0:1]:
                        scores(t + 1, m, (u + 1) % U)
                    aux_task(c)
                    for m in mine[1:2]:
                        scores(t + 1, m, (u + 1) % U)
                    if c % 2 == 1:
                        r, jj = c // 4 - 1, c // 2 % 2
                        if r >= 0 and runs(t):
                            values(t, r, jj, u)
                        if r < 0 and runs(t - 1):
                            values(t - 1, 3, jj, (u - 1) % U)
                    if c == 12 and runs(t - 2):
                        upto(pe, s_h2, t - 1)
                        upto(pe, s_mT, t + 1)
                        experts_out(t - 2)
                    for m in mine[2:3]:
                        scores(t + 1, m, (u + 1) % U)

            steps(pe, step)

        @block.vector
        def _(dve):
            n_set = [0]

            def link(ins):
                n_set[0] += 1
                ins.then_inc(s_set, 1)
                dve.wait_ge(s_set, n_set[0])

            link(dve.memset(zeros, 0.0))
            dve.memset(ones_sb[:], 1.0).then_inc(s_const, 1)
            dve.wait_ge(s_x, 16)
            link(dve.tensor_copy(xf, xi))
            link(dve.tensor_scalar(opens, xf, 40.0, None, ALU.is_equal))
            link(dve.scalar_tensor_tensor(opens, xf, 123.0, opens, ALU.is_equal, ALU.add))
            link(dve.scalar_tensor_tensor(opens, xf, 91.0, opens, ALU.is_equal, ALU.add))
            link(dve.tensor_scalar(closes, xf, 41.0, None, ALU.is_equal))
            link(dve.scalar_tensor_tensor(closes, xf, 125.0, closes, ALU.is_equal, ALU.add))
            link(dve.scalar_tensor_tensor(closes, xf, 93.0, closes, ALU.is_equal, ALU.add))
            link(dve.tensor_tensor(delta, opens, closes, ALU.subtract))
            link(dve.tensor_tensor_scan(depth, delta, zeros, 0.0, ALU.add, ALU.add))
            link(dve.tensor_tensor_scan(lowest, depth, zeros, 0.0, ALU.min, ALU.min))
            link(dve.tensor_tensor(depth, depth, lowest, ALU.subtract))
            dve.tensor_scalar(ids_sb[:, 0, :], depth, 0.0, float(NNEST - 1), ALU.max, ALU.min).then_inc(s_idset, 1)
            link(dve.tensor_scalar(xf, xf, 39990.0, None, ALU.is_gt))
            link(dve.tensor_tensor_scan(segi, xf, zeros, 0.0, ALU.add, ALU.add))
            link(dve.tensor_scalar(segi, segi, NSEG - 1, None, ALU.bitwise_and))
            dve.tensor_copy(ids_sb[:, 1, :], segi).then_inc(s_idset, 1)

            dve.wait_ge(s_w, 16 * 16)
            dve.tensor_copy(id16[:], id32[:]).then_inc(s_const, 1)
            dve.memset(eps_sb[:], EPS)
            dve.memset(minus_half[:], -0.5).then_inc(s_const, 1)
            dve.tensor_copy(kstk[STK:KROWS, 0, :, :],
                            const_sb[STK:KROWS, 4:4 + NH].unsqueeze(2).broadcast_to([3 * NH, NH, S])).then_inc(s_const, 1)
            dve.wait_ge(s_const, 4)
            for u in range(1, U):
                dve.tensor_copy(kstk[STK:KROWS, u, :, :], kstk[STK:KROWS, 0, :, :]).then_inc(s_const, 1)

            dve.wait_ge(s_setmm, 1)
            dve.tensor_copy(posW[:], aux_tiles).then_inc(s_setcp, 1)
            dve.wait_ge(s_setmm, 2)
            dve.tensor_copy(tab[:, 0, :], mx[0:HOT, 0, 0:P]).then_inc(s_setcp, 1)
            dve.wait_ge(s_setmm, 3)
            dve.tensor_copy(exp_w[:], mx[:, 1, 0:P]).then_inc(s_setcp, 1)
            dve.wait_ge(s_setmm, 4)
            dve.tensor_copy(obias[:], pv[:, 0:P]).then_inc(s_setcp, 1)

            dve.wait_ge(s_setcp, 2)
            link(dve.tensor_copy(tab16[:, 0, :], tab[:, 0, :]))
            link(dve.tensor_tensor(tab[:, 1, :], tab[:, 0, :], tab16[:, 0, :], ALU.subtract))
            link(dve.tensor_copy(tab16[:, 1, :], tab[:, 1, :]))
            link(dve.tensor_tensor(tab[:, 2, :], tab[:, 1, :], tab16[:, 1, :], ALU.subtract))
            link(dve.tensor_scalar(tab[:, 3, :], tab16[:, 0, :], const_sb[0:HOT, 1:2], None, ALU.mult))
            link(dve.scalar_tensor_tensor(tab[:, 0, :], tab16[:, 1, :], const_sb[0:HOT, 2:3], tab[:, 3, :],
                                          ALU.mult, ALU.add))
            dve.scalar_tensor_tensor(table[:], tab[:, 2, :], const_sb[0:HOT, 3:4], tab[:, 0, :],
                                     ALU.mult, ALU.add).then_inc(s_table, 1)

            def hot(b):
                upto(dve, s_ids, b, 32)
                upto(dve, s_embmm, b - 1)
                dve.tensor_scalar(onehot[:], ids_b[:], const_sb[0:HOT, 0:1], None, ALU.is_equal).then_inc(s_hot, 1)

            def add_pos(b):
                upto(dve, s_embmm, b)
                upto(dve, s_hb, b - 1)
                dve.tensor_tensor(h_sb[:], aux_tiles, posW[:], ALU.add).then_inc(s_h, 1)

            def stats(b, src, bn, mv, s_src, s_bn, s_mv):
                upto(dve, s_src, b)
                for j in range(NT):
                    dve.bn_stats(bn[:, j, :], src[:, j, :]).then_inc(s_bn, 1)
                upto(dve, s_bn, b, NT)
                dve.memset(after[:], 0.0)
                for j in range(NT):
                    dve.bn_aggr(mv[:, j, :], bn[:, j, :]).then_inc(s_mv, 1)

            def norm(b, src, mv, rs, dst, s_rs, s_dst, s_turned):
                upto(dve, s_rs, b)
                upto(dve, s_turned, b - 1)
                for j in range(NT):
                    dve.tensor_scalar(dst[:, j, :], src[:, j, :], mv[:, j, 0:1], rs[:, j:j + 1],
                                      ALU.subtract, ALU.mult).then_inc(s_dst, 1)

            def second(b, side):
                upto(dve, s_res0, b, 2, side + 1)
                upto(dve, s_pcout, b - 1, 96)
                dve.tensor_copy(pieces[:, side, 1, :], qkr[:, side, :]).then_inc(s_pc1, 1)

            def row_max(b, m):
                upto(dve, s_mxmm, b, 32, m + 1)
                dve.tensor_reduce(negmax[:, m // NT, m % NT:m % NT + 1], mx[:, m % 2, :], AX.X, ALU.max,
                                  negate=True).then_inc(s_max, 1)

            def cut_max(b):
                nm = negmax[:].rearrange("p h j -> p j h")
                upto(dve, s_max, b, 32)
                upto(dve, s_mTmm, b - 1)
                dve.tensor_copy(mpc[:, :, 0, :], nm).then_inc(s_mp, 1)
                upto(dve, s_mp, b, 4, 1)
                dve.tensor_tensor(mres[:], nm, mpc[:, :, 0, :], ALU.subtract).then_inc(s_mp, 1)
                upto(dve, s_mp, b, 4, 2)
                dve.tensor_copy(mpc[:, :, 1, :], mres[:]).then_inc(s_mp, 1)
                upto(dve, s_mp, b, 4, 3)
                dve.tensor_tensor(mpc[:, :, 2, :], mres[:], mpc[:, :, 1, :], ALU.subtract).then_inc(s_mp, 1)

            def invert_den(b):
                upto(dve, s_denin, b, 16)
                upto(dve, s_rdout, b - 1, 16)
                dve.reciprocal(rden[:], den[:]).then_inc(s_rden, 1)

            def add_attention(b, u):
                upto(dve, s_projmm, b)
                upto(dve, s_hb, b)
                dve.tensor_tensor(h2[:, u], aux_tiles, hb_sb[:, u], ALU.add).then_inc(s_h2, 1)

            def gate_first(b):
                upto(dve, s_gatTmm, b)
                dve.tensor_copy(logit[:], aux[:, 0:P].rearrange("p (j q) -> p j q", q=Q)[:, :, 0:5]).then_inc(s_logit, 1)
                upto(dve, s_logit, b)
                dve.tensor_reduce(lmax[:], logit[:, :, 0:NE], AX.X, ALU.max).then_inc(s_gate, 1)
                upto(dve, s_gate, b, 13, 1)
                dve.tensor_tensor(lsub[:, :, 0:NE], logit[:, :, 0:NE], lmax[:].unsqueeze(2).broadcast_to([P, NT, NE]),
                                  ALU.subtract).then_inc(s_gate, 1)
                dve.tensor_scalar(lsub[:, :, NE:NE + 1], logit[:, :, NE:NE + 1], -1.0, 87.0,
                                  ALU.mult, ALU.min).then_inc(s_gate, 1)

            def gate_second(b):
                upto(dve, s_gexp, b)
                dve.tensor_reduce(gden[:, :, 0:1], lexp[:, :, 0:NE], AX.X, ALU.add).then_inc(s_gate, 1)
                dve.tensor_scalar(gden[:, :, 1:2], lexp[:, :, NE:NE + 1], 1.0, None, ALU.add).then_inc(s_gate, 1)
                upto(dve, s_gate, b, 13, 5)
                dve.reciprocal(grec[:], gden[:]).then_inc(s_gate, 1)
                upto(dve, s_gate, b, 13, 6)
                dve.tensor_tensor(gsm[:], lexp[:, :, 0:NE], grec[:, :, 0:1].broadcast_to([P, NT, NE]),
                                  ALU.mult).then_inc(s_gate, 1)
                upto(dve, s_gate, b, 13, 7)
                dve.scalar_tensor_tensor(gad[:], grec[:, :, 1:2].broadcast_to([P, NT, NE]), -1.0 / NE, gsm[:],
                                         ALU.mult, ALU.add).then_inc(s_gate, 1)
                upto(dve, s_gate, b, 13, 8)
                dve.tensor_scalar(gsel[:], gad[:], 0.0, None, ALU.max).then_inc(s_gate, 1)
                upto(dve, s_gate, b, 13, 9)
                dve.tensor_reduce(wsum[:], gsel[:], AX.X, ALU.add).then_inc(s_gate, 1)
                upto(dve, s_gate, b, 13, 10)
                dve.scalar_tensor_tensor(wsafe[:], wsum[:], 0.0, wsum[:], ALU.is_equal, ALU.add).then_inc(s_gate, 1)
                upto(dve, s_gate, b, 13, 11)
                dve.reciprocal(wrec[:], wsafe[:]).then_inc(s_gate, 1)
                upto(dve, s_gate, b, 13, 12)
                upto(dve, s_wrow, b - 1)
                dve.tensor_tensor(wts[:], gsel[:], wrec[:].unsqueeze(2).broadcast_to([P, NT, NE]),
                                  ALU.mult).then_inc(s_gate, 1)

            def weigh(b):
                upto(dve, s_wTmm, b)
                upto(dve, s_outmm, b - 1)
                dve.tensor_tensor(low[:], lo_sb[:], aux[:], ALU.mult).then_inc(s_low, 1)

            def finish(b, u):
                upto(dve, s_outmm, b)
                upto(dve, s_store, b - 1, 16)
                dve.tensor_tensor(out_sb[:], aux_tiles, h2[:, u], ALU.add).then_inc(s_out, 1)

            def step(t, u):
                for c in range(SLOTS):
                    mine = [m for m in range(3 * c, min(3 * c + 3, 32))] if runs(t + 1) else []
                    for m in mine[0:1]:
                        row_max(t + 1, m)
                    if c == 0 and runs(t + 2):
                        add_pos(t + 2)
                    if c == 1 and runs(t - 2):
                        gate_first(t - 2)
                    if c == 4 and runs(t - 2):
                        gate_second(t - 2)
                    if c == 10 and runs(t - 2):
                        weigh(t - 2)
                    if c == 11 and runs(t + 1):
                        cut_max(t + 1)
                    if c == 11 and runs(t - 1):
                        add_attention(t - 1, (u - 1) % U)
                        stats(t - 1, h2[:, (u - 1) % U], bn2, mv2, s_h2, s_bn2, s_mv2)
                    if c == 12 and runs(t - 2):
                        finish(t - 2, (u - 2) % U)
                    if c == 12 and runs(t - 1):
                        norm(t - 1, h2[:, (u - 1) % U], mv2, rstd2, xn2, s_rstd2, s_xn2, s_xn2Tmm)
                    if c == 13 and runs(t + 3):
                        hot(t + 3)
                    for m in mine[1:2]:
                        row_max(t + 1, m)
                    if c == 0 and runs(t + 2):
                        stats(t + 2, h_sb, bn1, mv1, s_h, s_bn1, s_mv1)
                    if c == 1 and runs(t + 2):
                        norm(t + 2, h_sb, mv1, rstd1, xn, s_rstd1, s_xn, s_xnTmm)
                    if c in (5, 7) and runs(t + 2):
                        second(t + 2, (c - 5) // 2)
                    if c == 6 and runs(t - 1):
                        invert_den(t - 1)
                    for m in mine[2:3]:
                        row_max(t + 1, m)

            hot(0)
            steps(dve, step)


_INS = ["x", "posT", "catT", "consts", "ident", "tokW", "qkvT", "qkb", "bv", "ob", "woT", "wo_q", "gateT", "fc1T",
        "loA", "loBT", "fc2T"]


def kernel(**inputs):
    import numpy as np
    import concourse.bacc as bacc
    from concourse.bass_utils import run_bass_kernel_spmd

    a = {k.removeprefix("L0_"): np.asarray(v) for k, v in inputs.items()}
    f32 = np.float32

    nestT, segT = a["tok_nest_table"].T, a["tok_seg_table"].T
    catT = np.concatenate([nestT, nestT, nestT, np.zeros((P, SEGROW - 3 * NNEST), f32),
                           segT, segT, segT, np.zeros((P, HOT - SEGROW - 3 * NSEG), f32)], axis=1)
    qkv = a["attn_qkv_w"].reshape(NH, 3, HC, P)
    qkvb = a["attn_qkv_b"].reshape(NH, 3, HC)
    woT = a["attn_out_w"].T
    wo_q = np.zeros((4, Q, 2, P), f32)
    wo_q[:, 0:HC] = woT.reshape(2, 4, HC, P).transpose(1, 2, 0, 3)
    gateT = np.zeros((P, Q), f32)
    gateT[:, 0:NE] = a["ffn_gate_w"].T
    gateT[:, NE:NE + 1] = a["ffn_thr_w"].T
    loA = np.zeros((P, NE, Q), f32)
    loA[:, :, 0:NR] = a["ffn_lora_A"].transpose(1, 0, 2)
    loBT = np.zeros((P, NE, Q), f32)
    loBT[:, :, 0:NR] = a["ffn_lora_B"].transpose(2, 0, 1)

    consts = np.zeros((P, 4 + NH), f32)
    consts[:, 0] = -1
    for p in range(3):
        consts[p * NNEST:(p + 1) * NNEST, 0] = range(NNEST)
        consts[p * NNEST:(p + 1) * NNEST, 1 + p] = 1
        consts[SEGROW + p * NSEG:SEGROW + (p + 1) * NSEG, 0] = range(NSEG)
        consts[SEGROW + p * NSEG:SEGROW + (p + 1) * NSEG, 1 + p] = 1
        for h in range(NH):
            consts[STK + p * NH + h, 4 + h] = 1

    arrays = {
        "x": a["x"], "posT": a["tok_pos_table"].T, "catT": catT, "consts": consts, "ident": np.eye(P, dtype=f32),
        "tokW": a["tok_W"].reshape(3, P, P).transpose(1, 0, 2),
        "qkvT": qkv.transpose(3, 1, 0, 2).reshape(P, 3, P),
        "qkb": qkvb[:, 0:2].transpose(0, 2, 1).reshape(P, 2), "bv": qkvb[:, 2].reshape(P, 1),
        "ob": a["attn_out_b"].reshape(1, P), "woT": woT, "wo_q": wo_q.reshape(P, 2, P), "gateT": gateT,
        "fc1T": a["ffn_fc1_w"].transpose(2, 0, 1), "loA": loA, "loBT": loBT,
        "fc2T": a["ffn_fc2_w"].transpose(2, 0, 1),
    }
    arrays = {f"in_{k}": np.ascontiguousarray(v) for k, v in arrays.items()}

    nc = bacc.Bacc("TRN2", target_bir_lowering=False, num_devices=1)
    args = [nc.dram_tensor(f"in_{k}", arrays[f"in_{k}"].shape, mybir.dt.from_np(arrays[f"in_{k}"].dtype),
                           kind="ExternalInput").ap() for k in _INS]
    args.append(nc.dram_tensor("out", (NSEQ, S, P), F32, kind="ExternalOutput").ap())
    tower(nc, *args)
    r = run_bass_kernel_spmd(nc, [arrays], core_ids=[0])
    return r.results[0]["out"]
```

```python
from contextlib import ExitStack

import concourse.bass as bass
from concourse import mybir

ALU = mybir.AluOpType
ACT = mybir.ActivationFunctionType
AX = mybir.AxisListType
F32 = mybir.dt.float32
BF16 = mybir.dt.bfloat16
I32 = mybir.dt.int32

P = 128
NSEQ, S = 32, 512
NT = S // P
NH, HC = 8, 16
NE, NR = 4, 16
Q = 32
NNEST, NSEG = 16, 8
SEGROW = 64
HOT = 96
STK = 6 * HC
KROWS = STK + 3 * NH
SLOTS = 16
TILES = NH * NT
MSTART = 10
RING, MIX = 3, 4
PRODUCTS = ["q", "k", "v", "xn2T", "gates", "fc1_0", "fc1_1", "embed", "wT", "fc1_2", "fc1_3", "low", "mT", "xnT",
            "project", "out"]
U = 4
EPS = 1e-5
QSCALE = HC ** -0.5
Q_READS = [(0, 0, 3), (3 * HC, 0, 2), (5 * HC, 0, 1)]
K_READS = [(0, 0, 3), (3 * HC, 1, 2), (5 * HC, 2, 1)]


def tower(nc, x, posT, catT, consts, ident, tokW, qkvT, qkb, bv, ob, woT, wo_q, gateT, fc1T, loA, loBT, fc2T, out):
    nc.disable_value_cache = True
    ids_dram = nc.dram_tensor("ids_dram", (NSEQ, 2, S), BF16, kind="Internal").ap()
    stack_dram = nc.dram_tensor("stack_dram", (2, 3, HC, NH, S), BF16, kind="Internal").ap()
    den_dram = nc.dram_tensor("den_dram", (NH, S), F32, kind="Internal").ap()
    rden_dram = nc.dram_tensor("rden_dram", (2, 4, 2, S), F32, kind="Internal").ap()
    w_dram = nc.dram_tensor("w_dram", (NE, S), F32, kind="Internal").ap()

    with ExitStack() as ctx:
        def sb(name, shape, dt=F32):
            return ctx.enter_context(nc.sbuf_tensor(name, shape, dt))

        def sem(name):
            return ctx.enter_context(nc.semaphore(name))

        sc = ctx.enter_context(nc.psum_tensor("sc", [P, RING, S], F32))
        pv = ctx.enter_context(nc.psum_tensor("pv", [P, S], F32))
        mix = ctx.enter_context(nc.psum_tensor("mix", [P, MIX, S], F32))

        def aux(name, n=NT):
            bank = mix[:, (3 * PRODUCTS.index(name) + 1) % MIX]
            return bank if n == 1 else bank.rearrange("p (j n) -> p j n", j=n)

        def max_bank(m):
            return mix[:, (3 * ((MSTART + m // 2) % SLOTS) + 2 * (m % 2)) % MIX]


        probs = sb("probs", [P, 8, 2, S])
        posT_sb = probs[:, 6, 0, :]
        fc2T_sb = probs[:, 6, 1, :].rearrange("p (e n) -> p e n", e=NE)
        catT_sb = sb("catT_sb", [P, HOT])
        const_sb = sb("const_sb", [P, 4 + NH])
        id32 = sb("id32", [P, P])
        id16 = sb("id16", [P, P], BF16)
        tokW_sb = sb("tokW_sb", [P, 3, P])
        qkvT_sb = sb("qkvT_sb", [P, 3, P])
        qkb_sb = sb("qkb_sb", [P, 2])
        qb_sb = sb("qb_sb", [P, 1])
        bv_sb = sb("bv_sb", [P, 1])
        ob_sb = sb("ob_sb", [1, P])
        ones_sb = sb("ones_sb", [1, P])
        woT_sb = sb("woT_sb", [P, P])
        wo_q_sb = sb("wo_q_sb", [P, P])
        gateT_sb = sb("gateT_sb", [P, NE + 1])
        fc1T_sb = sb("fc1T_sb", [P, NE, P])
        loA_sb = sb("loA_sb", [P, NE, Q])
        loBT_sb = sb("loBT_sb", [P, NE, Q])
        exp_w = sb("exp_w", [P, P])
        posW = sb("posW", [P, NT, P])
        obias = sb("obias", [P, P])
        table = sb("table", [HOT, P], BF16)
        minus_half = sb("minus_half", [P, NT])
        eps_sb = sb("eps_sb", [P, NT])
        after = sb("after", [P, 1])

        xf, opens, closes, zeros, delta, depth, lowest = (probs[0:NSEQ, i // 2, i % 2, :] for i in range(7))
        xi, segi = (probs[0:NSEQ, 4, i, :].bitcast(I32) for i in range(2))
        ids_sb = sb("ids_sb", [NSEQ, 2, S], BF16)
        tab = probs[0:HOT, 7, 0, :].rearrange("p (i n) -> p i n", i=4)
        tab16 = sb("tab16", [HOT, 2, P], BF16)

        ids_b = sb("ids_b", [HOT, S], BF16)
        onehot = sb("onehot", [HOT, S], BF16)
        h_sb = sb("h_sb", [P, NT, P])
        hb_sb = sb("hb_sb", [P, U, NT, P])
        bn1 = sb("bn1", [P, NT, 6])
        mv1 = sb("mv1", [P, NT, 2])
        ve1 = sb("ve1", [P, NT])
        rstd1 = sb("rstd1", [P, NT])
        hc = sb("hc", [P, NT, P])
        xn = sb("xn", [P, NT, P])
        xnT = sb("xnT", [P, S])
        qk32 = sb("qk32", [P, 2, S])
        qkr = sb("qkr", [P, 2, S])
        pieces = sb("pieces", [P, 2, 3, S], BF16)
        vals = sb("vals", [P, U, NT, NH, Q])
        qstk = sb("qstk", [P, U, NH, S], BF16)
        kstk = sb("kstk", [P, U, NH, S], BF16)
        negmax = sb("negmax", [P, NH, NT])
        mres = sb("mres", [P, NT, NH])
        mpc = sb("mpc", [P, NT, 3, NH], BF16)
        mT = sb("mT", [3 * NH, S], BF16)
        ctx_sb = sb("ctx_sb", [P, 2, 2, S])
        den = sb("den", [P, Q])
        rden = sb("rden", [P, Q])
        rdenb = sb("rdenb", [P, 2, S])
        ctxh = sb("ctxh", [P, 2, S])
        ctxn = sb("ctxn", [P, S])
        h2 = sb("h2", [P, U, NT, P])
        bn2 = sb("bn2", [P, NT, 6])
        mv2 = sb("mv2", [P, NT, 2])
        ve2 = sb("ve2", [P, NT])
        rstd2 = sb("rstd2", [P, NT])
        xn2 = sb("xn2", [P, NT, P])
        xn2T = sb("xn2T", [P, S])
        logit = sb("logit", [P, NT, 5])
        lmax = sb("lmax", [P, NT])
        lsub = sb("lsub", [P, NT, 5])
        lexp = sb("lexp", [P, NT, 5])
        gden = sb("gden", [P, NT, 2])
        grec = sb("grec", [P, NT, 2])
        gsm = sb("gsm", [P, NT, NE])
        gad = sb("gad", [P, NT, NE])
        gsel = sb("gsel", [P, NT, NE])
        wsum = sb("wsum", [P, NT])
        wsafe = sb("wsafe", [P, NT])
        wrec = sb("wrec", [P, NT])
        wts = sb("wts", [P, NT, NE])
        wT = sb("wT", [NT * NE, P])
        wrow = sb("wrow", [P, S])
        hid = sb("hid", [P, NE, S])
        low = sb("low", [P, S])
        out_sb = sb("out_sb", [P, NT, P])

        s_x = sem("s_x")
        s_w = sem("s_w")
        s_set = sem("s_set")
        s_setmm = sem("s_setmm")
        s_setcp = sem("s_setcp")
        s_idset = sem("s_idset")
        s_qb = sem("s_qb")
        s_table = sem("s_table")
        s_idsout = sem("s_idsout")
        s_const = sem("s_const")
        s_pconst = sem("s_pconst")
        s_ids = sem("s_ids")
        s_hot = sem("s_hot")
        s_embmm, s_h, s_hb = sem("s_embmm"), sem("s_h"), sem("s_hb")
        s_bn1, s_mv1, s_ve1, s_rstd1, s_hc, s_xn = (sem(n) for n in ("s_bn1", "s_mv1", "s_ve1", "s_rstd1", "s_hc", "s_xn"))
        s_xnTmm, s_xnT = sem("s_xnTmm"), sem("s_xnT")
        s_qmm, s_kmm, s_vmm = sem("s_qmm"), sem("s_kmm"), sem("s_vmm")
        s_qk32 = sem("s_qk32")
        s_v = sem("s_v")
        s_pc0, s_res0, s_pc1, s_pc2 = sem("s_pc0"), sem("s_res0"), sem("s_pc1"), sem("s_pc2")
        s_pcout = [sem(f"s_pcout{a}") for a in "qk"]
        s_stk = [sem(f"s_stk{a}") for a in "qk"]
        s_mxmm, s_max = sem("s_mxmm"), sem("s_max")
        s_mp = sem("s_mp")
        s_mTmm, s_mT, s_mrow = sem("s_mTmm"), sem("s_mT"), sem("s_mrow")
        s_score, s_exp, s_pv, s_ctx = sem("s_score"), sem("s_exp"), sem("s_pv"), sem("s_ctx")
        s_denout, s_denin, s_rden, s_rdout = sem("s_denout"), sem("s_denin"), sem("s_rden"), sem("s_rdout")
        s_rdin = [sem(f"s_rdin{g}") for g in range(2)]
        s_ctxh, s_ctxn = sem("s_ctxh"), sem("s_ctxn")
        s_zrow = sem("s_zrow")
        s_projmm, s_h2 = sem("s_projmm"), sem("s_h2")
        s_bn2, s_mv2, s_ve2, s_rstd2, s_xn2 = sem("s_bn2"), sem("s_mv2"), sem("s_ve2"), sem("s_rstd2"), sem("s_xn2")
        s_xn2Tmm, s_xn2T = sem("s_xn2Tmm"), sem("s_xn2T")
        s_gatmm, s_logit = sem("s_gatmm"), sem("s_logit")
        s_gate = sem("s_gate")
        s_gexp = sem("s_gexp")
        s_wTmm, s_wT, s_wout, s_win = sem("s_wTmm"), sem("s_wT"), sem("s_wout"), sem("s_win")
        s_fc1mm, s_hid = sem("s_fc1mm"), sem("s_hid")
        s_lomm, s_low = sem("s_lomm"), sem("s_low")
        s_outmm, s_out, s_store = sem("s_outmm"), sem("s_out"), sem("s_store")

        def upto(eng, s, b, per=1, k=None):
            k = per if k is None else k
            if isinstance(b, int):
                value = min(per * b + k, per * NSEQ)
                if value > 0:
                    eng.wait_ge(s, value)
            else:
                eng.wait_ge(s, b * per + k)

        def ring_free(eng, s, b, i):
            upto(eng, s, b, TILES, i - RING + 1 if i >= RING else min(i - 1, 0))

        def runs(b):
            return not isinstance(b, int) or 0 <= b < NSEQ

        def steps(eng, step):
            first = 3
            rounds = (NSEQ - 3 - first) // U
            for t in range(-3, first):
                step(t, t % U)
            with eng.Fori(0, rounds) as i:
                for u in range(U):
                    step(eng.snap(i * U + (first + u)), (first + u) % U)
            for t in range(first + rounds * U, NSEQ + 2):
                step(t, t % U)

        block = ctx.enter_context(nc.Block())

        @block.sync
        def _(sp):
            sp.dma_start(xi, x).then_inc(s_x, 16)
            for dst, src in [(const_sb[:], consts), (id32[:], ident), (catT_sb[:], catT),
                             (tokW_sb[:], tokW), (posT_sb, posT), (qkvT_sb[:], qkvT), (qkb_sb[:], qkb),
                             (bv_sb[:], bv), (ob_sb[:], ob), (woT_sb[:], woT), (wo_q_sb[:], wo_q),
                             (gateT_sb[:], gateT), (fc1T_sb[:], fc1T), (loA_sb[:], loA), (loBT_sb[:], loBT),
                             (fc2T_sb, fc2T)]:
                sp.dma_start(dst, src).then_inc(s_w, 16)
            sp.wait_ge(s_idset, 2)
            sp.dma_start(ids_dram, ids_sb[:]).then_inc(s_idsout, 16)
            for g in range(2):
                sp.dma_start(rden_dram[g, :, 1 - g], zeros[0:4, :]).then_inc(s_zrow, 16)
            sp.wait_ge(s_idsout, 16)
            sp.wait_ge(s_zrow, 32)

            def load_ids(b):
                upto(sp, s_hot, b - 1)
                sp.dma_start(ids_b[0:SEGROW, :], ids_dram[b, 0].partition_broadcast(SEGROW)).then_inc(s_ids, 16)
                sp.dma_start(ids_b[SEGROW:HOT, :], ids_dram[b, 1].partition_broadcast(HOT - SEGROW)).then_inc(s_ids, 16)

            def store_piece(b, side, p):
                upto(sp, (s_pc0, s_pc1, s_pc2)[p], b, 2, side + 1)
                if p == 0:
                    upto(sp, s_stk[side], b - 1, 48)
                sp.dma_start(stack_dram[side, p].rearrange("c h s -> h c s"),
                             pieces[:, side, p, :]).then_inc(s_pcout[side], 16)

            def load_qstack(b, u):
                upto(sp, s_pcout[0], b, 48)
                upto(sp, s_score, b - U, TILES)
                for row, p, n in Q_READS:
                    sp.dma_start(qstk[row:row + n * HC, u, :, :],
                                 stack_dram[0, p:p + n].rearrange("p c h s -> (p c) h s")).then_inc(s_stk[0], 16)

            def load_kstack(b, u):
                upto(sp, s_pcout[1], b, 48)
                upto(sp, s_score, b - U, TILES)
                for row, p, n in K_READS:
                    sp.dma_start(kstk[row:row + n * HC, u, :, :],
                                 stack_dram[1, p].unsqueeze(0).broadcast_to([n, HC, NH, S])).then_inc(s_stk[1], 16)

            def load_max(b, u):
                upto(sp, s_mT, b)
                sp.dma_start(qstk[STK:KROWS, u, :, :],
                             mT[:].unsqueeze(1).broadcast_to([3 * NH, NH, S])).then_inc(s_mrow, 16)

            def store_den(b, g, u):
                upto(sp, s_ctx, b, 2, g + 1)
                upto(sp, s_denin, b - 1, 16)
                row = (HC, 0)[g]
                sp.dma_start(den_dram[4 * g:4 * g + 4], ctx_sb[row:P:Q, u % 2, g, :]).then_inc(s_denout, 16)

            def load_den(b):
                upto(sp, s_denout, b, 32)
                upto(sp, s_rden, b - 1)
                sp.dma_start(den[:], den_dram.rearrange("h (k s) -> (h k) s", s=Q)).then_inc(s_denin, 16)

            def store_rden(b):
                for g in range(2):
                    upto(sp, s_rdin[g], b - 1, 16)
                upto(sp, s_rden, b)
                for g in range(2):
                    sp.dma_start(rden_dram[g, :, g].rearrange("q (k s) -> q k s", s=Q),
                                 rden[64 * g:64 * g + 64, :]).then_inc(s_rdout, 16)

            def load_rden(b):
                for g in range(2):
                    upto(sp, s_ctxh, b - 1, 2, g + 1)
                    if g == 0:
                        upto(sp, s_rdout, b, 32)
                    sp.dma_start(rdenb[:, g, :],
                                 rden_dram[g].rearrange("q a s -> (q a) s").unsqueeze(1).broadcast_to([8, HC, S])
                                 ).then_inc(s_rdin[g], 16)

            def store_weights(b):
                upto(sp, s_wT, b)
                upto(sp, s_win, b - 1, 16)
                sp.dma_start(w_dram.rearrange("e (j n) -> j e n", n=P), wT[:]).then_inc(s_wout, 16)

            def load_weights(b):
                upto(sp, s_low, b - 1)
                upto(sp, s_wout, b, 16)
                sp.dma_start(wrow[:], w_dram.unsqueeze(1).broadcast_to([NE, Q, S])).then_inc(s_win, 16)

            def store_out(b):
                upto(sp, s_out, b)
                sp.dma_start(out[b].rearrange("(j p) d -> p j d", p=P), out_sb[:]).then_inc(s_store, 16)

            def step(t, u):
                if runs(t + 3):
                    load_ids(t + 3)
                if runs(t + 2):
                    store_piece(t + 2, 0, 0)
                    store_piece(t + 2, 1, 0)
                    store_piece(t + 2, 0, 1)
                if runs(t - 1):
                    store_den(t - 1, 1, (u - 1) % U)
                if runs(t + 2):
                    store_piece(t + 2, 1, 1)
                    store_piece(t + 2, 0, 2)
                if runs(t - 1):
                    load_den(t - 1)
                if runs(t + 2):
                    store_piece(t + 2, 1, 2)
                    load_qstack(t + 2, (u + 2) % U)
                    load_kstack(t + 2, (u + 2) % U)
                if runs(t - 1):
                    store_rden(t - 1)
                if runs(t - 2):
                    store_weights(t - 2)
                if runs(t - 1):
                    load_rden(t - 1)
                if runs(t - 2):
                    load_weights(t - 2)
                if runs(t):
                    store_den(t, 0, u)
                if runs(t + 1):
                    load_max(t + 1, (u + 1) % U)
                if runs(t - 2):
                    store_out(t - 2)

            steps(sp, step)
            sp.wait_ge(s_store, 16 * NSEQ)

        @block.gpsimd
        def _(pool):
            pool.wait_ge(s_w, 16 * 16)
            for v in range(U):
                pool.memset(vals[:, v, :, 0:4, HC:Q], 1.0).then_inc(s_pconst, 1)
                pool.memset(vals[:, v, :, 4:NH, 0:HC], 1.0).then_inc(s_pconst, 1)

            def rstd(b, mv, ve, rs, s_mv, s_ve, s_rs, s_used, n_used):
                upto(pool, s_mv, b, NT)
                upto(pool, s_used, b - 1, n_used)
                pool.tensor_tensor(ve[:], mv[:, :, 1], eps_sb[:], ALU.add).then_inc(s_ve, 1)
                upto(pool, s_ve, b)
                pool.tensor_tensor(rs[:], ve[:], minus_half[:], ALU.pow).then_inc(s_rs, 1)

            def add_bias(b, u):
                upto(pool, s_h, b)
                upto(pool, s_h2, b - U)
                pool.tensor_tensor(hb_sb[:, u], h_sb[:], obias[:].unsqueeze(1).broadcast_to([P, NT, P]),
                                   ALU.add).then_inc(s_hb, 1)

            def residual(b, side):
                upto(pool, s_pc0, b, 2, side + 1)
                pool.tensor_tensor(qkr[:, side, :], qk32[:, side, :], pieces[:, side, 0, :],
                                   ALU.subtract).then_inc(s_res0, 1)

            def third(b, side):
                upto(pool, s_pc1, b, 2, side + 1)
                upto(pool, s_pcout[side], b - 1, 48)
                pool.tensor_tensor(pieces[:, side, 2, :], qkr[:, side, :], pieces[:, side, 1, :],
                                   ALU.subtract).then_inc(s_pc2, 1)

            def norm(b):
                upto(pool, s_rstd1, b)
                pool.tensor_tensor(hc[:], h_sb[:], mv1[:, :, 0:1].broadcast_to([P, NT, P]),
                                   ALU.subtract).then_inc(s_hc, 1)
                upto(pool, s_hc, b)
                upto(pool, s_xnTmm, b - 1)
                pool.tensor_tensor(xn[:], hc[:], rstd1[:].unsqueeze(2).broadcast_to([P, NT, P]),
                                   ALU.mult).then_inc(s_xn, 1)

            def normalise(b, u):
                for g in range(2):
                    upto(pool, s_rdin[g], b, 16)
                    pool.tensor_tensor(ctxh[:, g, :], ctx_sb[:, u % 2, g, :], rdenb[:, g, :],
                                       ALU.mult).then_inc(s_ctxh, 1)
                upto(pool, s_ctxh, b, 2)
                upto(pool, s_projmm, b - 1)
                pool.tensor_tensor(ctxn[:], ctxh[:, 0, :], ctxh[:, 1, :], ALU.add).then_inc(s_ctxn, 1)

            pool.wait_ge(s_setcp, 4)
            pool.wait_ge(s_const, 3)

            def step(t, u):
                if runs(t - 2):
                    rstd(t - 2, mv2, ve2, rstd2, s_mv2, s_ve2, s_rstd2, s_xn2, NT)
                if runs(t + 2):
                    residual(t + 2, 0)
                    residual(t + 2, 1)
                    add_bias(t + 2, (u + 2) % U)
                    third(t + 2, 0)
                    third(t + 2, 1)
                if runs(t + 3):
                    rstd(t + 3, mv1, ve1, rstd1, s_mv1, s_ve1, s_rstd1, s_xn, 1)
                    norm(t + 3)
                if runs(t - 1):
                    normalise(t - 1, (u - 1) % U)

            steps(pool, step)

        @block.scalar
        def _(act):
            act.wait_ge(s_w, 16 * 16)
            act.mul(qb_sb[:], qkb_sb[:, 0:1], QSCALE).then_inc(s_qb, 1)
            act.wait_ge(s_qb, 1)

            def exp(b, i):
                c = i // 2
                upto(act, s_score, b, TILES, i + 1)
                if i % 8 == 0:
                    upto(act, s_pv, b, 8, 2 * (c // 4) - 2)
                act.activation(probs[:, c % 8, i % 2], sc[:, i % RING], ACT.Exp).then_inc(s_exp, 1)

            def copy_xnT(b):
                upto(act, s_xnTmm, b)
                upto(act, s_vmm, b - 1)
                act.copy(xnT[:], aux("xnT", 1)).then_inc(s_xnT, 1)

            def copy_qk(b, side):
                upto(act, (s_qmm, s_kmm)[side], b)
                upto(act, s_res0, b - 1, 2, side + 1)
                act.activation(qk32[:, side, :], aux("qk"[side], 1), ACT.Identity,
                               bias=(qb_sb[:], qkb_sb[:, 1:2])[side], scale=(QSCALE, 1.0)[side]).then_inc(s_qk32, 1)
                upto(act, s_qk32, b, 2, side + 1)
                upto(act, s_pcout[side], b - 1, 48)
                act.copy(pieces[:, side, 0, :], qk32[:, side, :]).then_inc(s_pc0, 1)

            def copy_v(b, u):
                upto(act, s_vmm, b)
                upto(act, s_pv, b - U, 8)
                v = aux("v", 1).rearrange("p (j h c) -> p j h c", j=NT, h=NH)
                act.copy(vals[:, u, :, 0:4, 0:HC], v[:, :, 0:4]).then_inc(s_v, 1)
                act.copy(vals[:, u, :, 4:NH, HC:Q], v[:, :, 4:NH]).then_inc(s_v, 1)

            def copy_mT(b):
                upto(act, s_mTmm, b)
                upto(act, s_mrow, b - 1, 16)
                act.copy(mT[:], aux("mT", 1)[0:3 * NH]).then_inc(s_mT, 1)

            def copy_ctx(b, g, u):
                upto(act, s_pv, b, 8, 4 * g + 4)
                upto(act, s_ctxh, b - 2, 2, g + 1)
                upto(act, s_denout, b - 2, 32)
                act.copy(ctx_sb[:, u % 2, g, :], pv[:]).then_inc(s_ctx, 1)

            def copy_xn2T(b):
                upto(act, s_xn2Tmm, b)
                upto(act, s_fc1mm, b - 1, NE)
                act.copy(xn2T[:], aux("xn2T", 1)).then_inc(s_xn2T, 1)

            def gate_exp(b):
                upto(act, s_gate, b, 13, 3)
                upto(act, s_gate, b - 1, 13, 7)
                act.activation(lexp[:], lsub[:], ACT.Exp).then_inc(s_gexp, 1)

            def copy_wT(b):
                upto(act, s_wTmm, b)
                upto(act, s_wout, b - 1, 16)
                act.copy(wT[:], aux("wT", 1)[0:NT * NE, 0:P]).then_inc(s_wT, 1)

            def relu(b, e):
                upto(act, s_fc1mm, b, NE, e + 1)
                upto(act, s_lomm, b - 1)
                act.activation(hid[:, e, :], aux(f"fc1_{e}", 1), ACT.Relu).then_inc(s_hid, 1)

            def step(t, u):
                for c in range(SLOTS):
                    if runs(t):
                        exp(t, 2 * c)
                        exp(t, 2 * c + 1)
                    now = PRODUCTS[c]
                    if now in ("q", "k") and runs(t + 2):
                        copy_qk(t + 2, c)
                    if now == "v" and runs(t + 2):
                        copy_v(t + 2, (u + 2) % U)
                    if now == "xn2T" and runs(t - 2):
                        copy_xn2T(t - 2)
                    if c == 3 and runs(t - 1):
                        copy_ctx(t - 1, 1, (u - 1) % U)
                    if c == 5 and runs(t - 2):
                        gate_exp(t - 2)
                    if now.startswith("fc1") and runs(t - 2):
                        relu(t - 2, int(now[-1]))
                    if now == "wT" and runs(t - 2):
                        copy_wT(t - 2)
                    if c == 11 and runs(t):
                        copy_ctx(t, 0, u)
                    if now == "mT" and runs(t + 1):
                        copy_mT(t + 1)
                    if now == "xnT" and runs(t + 3):
                        copy_xnT(t + 3)

            steps(act, step)

        @block.tensor
        def _(pe):
            pe.wait_ge(s_w, 16 * 16)
            pe.wait_ge(s_const, 2)

            for j in range(NT):
                mm = pe.matmul(mix[:, 0, j * P:(j + 1) * P], posT_sb[:, j * P:(j + 1) * P], tokW_sb[:, 0, :], start=True, stop=True)
            mm.then_inc(s_setmm, 1)
            pe.matmul(mix[0:SEGROW, 1, 0:P], catT_sb[:, 0:SEGROW], tokW_sb[:, 1, :], start=True, stop=True)
            pe.matmul(mix[SEGROW:HOT, 1, 0:P], catT_sb[:, SEGROW:HOT], tokW_sb[:, 2, :], start=True, stop=True).then_inc(s_setmm, 1)
            for e in range(NE):
                mm = pe.matmul(mix[Q * e:Q * e + Q, 2, 0:P], loBT_sb[:, e, :], fc2T_sb[:, e, :], start=True, stop=True)
            mm.then_inc(s_setmm, 1)
            pe.matmul(pv[:, 0:P], bv_sb[:].broadcast_to([P, P]), woT_sb[:], start=True, stop=False)
            pe.matmul(pv[:, 0:P], ones_sb[:], ob_sb[:], start=False, stop=True).then_inc(s_setmm, 1)
            pe.wait_ge(s_setcp, 4)
            pe.wait_ge(s_table, 1)
            pe.wait_ge(s_pconst, 2 * U)
            pe.wait_ge(s_const, 3 + U)

            def scores_T(b, i, u):
                c, g = i // 2, i // 16
                half, h = c // 4 % 2, 4 * g + c % 4
                j = 2 * half + i % 2
                if i == 0:
                    upto(pe, s_mrow, b, 16)
                ring_free(pe, s_exp, b, i)
                pe.matmul(sc[:, i % RING, :], kstk[0:KROWS, u, h, j * P:(j + 1) * P],
                          qstk[0:KROWS, u, h, :], start=True, stop=True).then_inc(s_score, 1)

            def values(b, r, jj, u):
                g, half = r // 2, r % 2
                if jj == 0:
                    upto(pe, s_exp, b, TILES, 8 * r + 8)
                    if half == 0:
                        upto(pe, s_ctx, b, 2, g)
                for i in range(4):
                    mm = pe.matmul(pv[Q * i:Q * i + Q, :], vals[:, u, 2 * half + jj, 4 * g + i, :],
                                   probs[:, 4 * (r % 2) + i, jj, :],
                                   start=(half == 0 and jj == 0), stop=(half == 1 and jj == 1))
                mm.then_inc(s_pv, 1)

            def scores(b, m, u):
                h, j = m // NT, m % NT
                if m == 0:
                    for side in range(2):
                        upto(pe, s_stk[side], b, 48)
                pe.matmul(max_bank(m), qstk[0:STK, u, h, j * P:(j + 1) * P],
                          kstk[0:STK, u, h, :], start=True, stop=True).then_inc(s_mxmm, 1)

            def embed(b):
                upto(pe, s_hot, b)
                for j in range(NT):
                    mm = pe.matmul(aux("embed")[:, j, :], onehot[:, j * P:(j + 1) * P], table[:], start=True, stop=True)
                mm.then_inc(s_embmm, 1)

            def turn(b, name, src, ready, n_ready, signal):
                upto(pe, ready, b, n_ready)
                for j in range(NT):
                    mm = pe.transpose(aux(name)[:, j, :], src[:, j, :], id32[:])
                mm.then_inc(signal, 1)

            def qk(b, side):
                upto(pe, s_xnT, b)
                pe.matmul(aux("qk"[side], 1), qkvT_sb[:, side, :], xnT[:], start=True, stop=True).then_inc((s_qmm, s_kmm)[side], 1)

            def v(b):
                for j in range(NT):
                    mm = pe.matmul(aux("v")[:, j, :], xnT[:, j * P:(j + 1) * P], qkvT_sb[:, 2, :], start=True, stop=True)
                mm.then_inc(s_vmm, 1)

            def turn_max(b):
                upto(pe, s_mp, b, 4)
                for j in range(NT):
                    mm = pe.matmul(aux("mT")[0:3 * NH, j, :], mpc[:, j].rearrange("p a h -> p (a h)"), id16[:],
                                   start=True, stop=True)
                mm.then_inc(s_mTmm, 1)

            def project(b):
                upto(pe, s_ctxn, b)
                for j in range(NT):
                    mm = pe.matmul(aux("project")[:, j, :], ctxn[:, j * P:(j + 1) * P], wo_q_sb[:], start=True, stop=True)
                mm.then_inc(s_projmm, 1)

            def gates(b):
                upto(pe, s_xn2T, b)
                for j in range(NT):
                    mm = pe.matmul(aux("gates")[:, j, 0:NE + 1], xn2T[:, j * P:(j + 1) * P], gateT_sb[:],
                                   start=True, stop=True)
                mm.then_inc(s_gatmm, 1)

            def fc1(b, e):
                pe.matmul(aux(f"fc1_{e}", 1), fc1T_sb[:, e, :], xn2T[:], start=True, stop=True).then_inc(s_fc1mm, 1)

            def low_rank(b):
                upto(pe, s_hid, b, NE)
                for e in range(NE):
                    mm = pe.matmul(aux("low", 1)[Q * e:Q * e + Q], loA_sb[:, e, :], hid[:, e, :], start=True, stop=True)
                mm.then_inc(s_lomm, 1)

            def turn_weights(b):
                upto(pe, s_gate, b, 13)
                pe.transpose(aux("wT", 1)[0:NT * NE, 0:P], wts[:].rearrange("p j e -> p (j e)"), id32[:]).then_inc(s_wTmm, 1)

            def experts_out(b):
                upto(pe, s_low, b)
                for j in range(NT):
                    mm = pe.matmul(aux("out")[:, j, :], low[:, j * P:(j + 1) * P], exp_w[:], start=True, stop=True)
                mm.then_inc(s_outmm, 1)

            products = {
                "q": (2, lambda b: qk(b, 0), (s_qk32, 2, 1)),
                "k": (2, lambda b: qk(b, 1), (s_qk32, 2, 2)),
                "v": (2, v, (s_v, 2, 2)),
                "xn2T": (-2, lambda b: turn(b, "xn2T", xn2, s_xn2, NT, s_xn2Tmm), (s_xn2T, 1, 1)),
                "gates": (-2, gates, (s_logit, 1, 1)),
                "fc1_0": (-2, lambda b: fc1(b, 0), (s_hid, NE, 1)),
                "fc1_1": (-2, lambda b: fc1(b, 1), (s_hid, NE, 2)),
                "wT": (-2, turn_weights, (s_wT, 1, 1)),
                "fc1_2": (-2, lambda b: fc1(b, 2), (s_hid, NE, 3)),
                "fc1_3": (-2, lambda b: fc1(b, 3), (s_hid, NE, 4)),
                "embed": (3, embed, (s_h, 1, 1)),
                "low": (-2, low_rank, (s_low, 1, 1)),
                "mT": (1, turn_max, (s_mT, 1, 1)),
                "xnT": (3, lambda b: turn(b, "xnT", xn, s_xn, 1, s_xnTmm), (s_xnT, 1, 1)),
                "project": (-1, project, (s_h2, 1, 1)),
                "out": (-2, experts_out, (s_out, 1, 1)),
            }

            def mix_user(t, n):
                t, c, kind = t + n // (3 * SLOTS), n // 3 % SLOTS, n % 3
                if kind == 1:
                    ahead, _, read = products[PRODUCTS[c]]
                    return t + ahead, read
                return t + (2 if c >= MSTART else 1), (s_max, TILES, 2 * ((c - MSTART) % SLOTS) + kind // 2 + 1)

            def mix_free(t, n):
                for before in range(n - MIX, -6 * SLOTS, -MIX):
                    b, (read, per, k) = mix_user(t, before)
                    if runs(b):
                        upto(pe, read, b, per, k)
                        return

            def row_tile(t, u, c, i):
                ahead = 2 if c >= MSTART else 1
                if runs(t + ahead):
                    mix_free(t, 3 * c + 2 * i)
                    scores(t + ahead, 2 * ((c - MSTART) % SLOTS) + i, (u + ahead) % U)

            def product(t, c):
                ahead, compute, _ = products[PRODUCTS[c]]
                if runs(t + ahead):
                    mix_free(t, 3 * c + 1)
                    compute(t + ahead)

            def step(t, u):
                for c in range(SLOTS):
                    if runs(t):
                        scores_T(t, 2 * c, u)
                        scores_T(t, 2 * c + 1, u)
                    row_tile(t, u, c, 0)
                    product(t, c)
                    row_tile(t, u, c, 1)
                    if c % 2 == 1:
                        r, jj = c // 4 - 1, c // 2 % 2
                        if r >= 0 and runs(t):
                            values(t, r, jj, u)
                        if r < 0 and runs(t - 1):
                            values(t - 1, 3, jj, (u - 1) % U)

            steps(pe, step)

        @block.vector
        def _(dve):
            n_set = [0]

            def link(ins):
                n_set[0] += 1
                ins.then_inc(s_set, 1)
                dve.wait_ge(s_set, n_set[0])

            link(dve.memset(zeros, 0.0))
            dve.memset(ones_sb[:], 1.0).then_inc(s_const, 1)
            dve.wait_ge(s_x, 16)
            link(dve.tensor_copy(xf, xi))
            link(dve.tensor_scalar(opens, xf, 40.0, None, ALU.is_equal))
            link(dve.scalar_tensor_tensor(opens, xf, 123.0, opens, ALU.is_equal, ALU.add))
            link(dve.scalar_tensor_tensor(opens, xf, 91.0, opens, ALU.is_equal, ALU.add))
            link(dve.tensor_scalar(closes, xf, 41.0, None, ALU.is_equal))
            link(dve.scalar_tensor_tensor(closes, xf, 125.0, closes, ALU.is_equal, ALU.add))
            link(dve.scalar_tensor_tensor(closes, xf, 93.0, closes, ALU.is_equal, ALU.add))
            link(dve.tensor_tensor(delta, opens, closes, ALU.subtract))
            link(dve.tensor_tensor_scan(depth, delta, zeros, 0.0, ALU.add, ALU.add))
            link(dve.tensor_tensor_scan(lowest, depth, zeros, 0.0, ALU.min, ALU.min))
            link(dve.tensor_tensor(depth, depth, lowest, ALU.subtract))
            dve.tensor_scalar(ids_sb[:, 0, :], depth, 0.0, float(NNEST - 1), ALU.max, ALU.min).then_inc(s_idset, 1)
            link(dve.tensor_scalar(xf, xf, 39990.0, None, ALU.is_gt))
            link(dve.tensor_tensor_scan(segi, xf, zeros, 0.0, ALU.add, ALU.add))
            link(dve.tensor_scalar(segi, segi, NSEG - 1, None, ALU.bitwise_and))
            dve.tensor_copy(ids_sb[:, 1, :], segi).then_inc(s_idset, 1)

            dve.wait_ge(s_w, 16 * 16)
            dve.tensor_copy(id16[:], id32[:]).then_inc(s_const, 1)
            dve.memset(eps_sb[:], EPS)
            dve.memset(minus_half[:], -0.5).then_inc(s_const, 1)
            dve.tensor_copy(kstk[STK:KROWS, 0, :, :],
                            const_sb[STK:KROWS, 4:4 + NH].unsqueeze(2).broadcast_to([3 * NH, NH, S])).then_inc(s_const, 1)
            dve.wait_ge(s_const, 4)
            for u in range(1, U):
                dve.tensor_copy(kstk[STK:KROWS, u, :, :], kstk[STK:KROWS, 0, :, :]).then_inc(s_const, 1)

            dve.wait_ge(s_setmm, 1)
            dve.tensor_copy(posW[:], mix[:, 0].rearrange("p (j n) -> p j n", j=NT)).then_inc(s_setcp, 1)
            dve.wait_ge(s_setmm, 2)
            dve.tensor_copy(tab[:, 0, :], mix[0:HOT, 1, 0:P]).then_inc(s_setcp, 1)
            dve.wait_ge(s_setmm, 3)
            dve.tensor_copy(exp_w[:], mix[:, 2, 0:P]).then_inc(s_setcp, 1)
            dve.wait_ge(s_setmm, 4)
            dve.tensor_copy(obias[:], pv[:, 0:P]).then_inc(s_setcp, 1)

            dve.wait_ge(s_setcp, 2)
            link(dve.tensor_copy(tab16[:, 0, :], tab[:, 0, :]))
            link(dve.tensor_tensor(tab[:, 1, :], tab[:, 0, :], tab16[:, 0, :], ALU.subtract))
            link(dve.tensor_copy(tab16[:, 1, :], tab[:, 1, :]))
            link(dve.tensor_tensor(tab[:, 2, :], tab[:, 1, :], tab16[:, 1, :], ALU.subtract))
            link(dve.tensor_scalar(tab[:, 3, :], tab16[:, 0, :], const_sb[0:HOT, 1:2], None, ALU.mult))
            link(dve.scalar_tensor_tensor(tab[:, 0, :], tab16[:, 1, :], const_sb[0:HOT, 2:3], tab[:, 3, :],
                                          ALU.mult, ALU.add))
            dve.scalar_tensor_tensor(table[:], tab[:, 2, :], const_sb[0:HOT, 3:4], tab[:, 0, :],
                                     ALU.mult, ALU.add).then_inc(s_table, 1)

            def hot(b):
                upto(dve, s_ids, b, 32)
                upto(dve, s_embmm, b - 1)
                dve.tensor_scalar(onehot[:], ids_b[:], const_sb[0:HOT, 0:1], None, ALU.is_equal).then_inc(s_hot, 1)

            def add_pos(b):
                upto(dve, s_embmm, b)
                upto(dve, s_hb, b - 1)
                upto(dve, s_hc, b - 1)
                dve.tensor_tensor(h_sb[:], aux("embed"), posW[:], ALU.add).then_inc(s_h, 1)

            def stats(b, src, bn, s_src, s_bn):
                upto(dve, s_src, b)
                for j in range(NT):
                    dve.bn_stats(bn[:, j, :], src[:, j, :]).then_inc(s_bn, 1)

            def moments(b, bn, mv, s_bn, s_mv):
                upto(dve, s_bn, b, NT)
                dve.memset(after[:], 0.0)
                for j in range(NT):
                    dve.bn_aggr(mv[:, j, :], bn[:, j, :]).then_inc(s_mv, 1)

            def norm2(b, u, tiles):
                upto(dve, s_rstd2, b)
                upto(dve, s_xn2Tmm, b - 1)
                for j in tiles:
                    dve.tensor_scalar(xn2[:, j, :], h2[:, u, j, :], mv2[:, j, 0:1], rstd2[:, j:j + 1],
                                      ALU.subtract, ALU.mult).then_inc(s_xn2, 1)

            def second(b, side):
                upto(dve, s_res0, b, 2, side + 1)
                upto(dve, s_pcout[side], b - 1, 48)
                dve.tensor_copy(pieces[:, side, 1, :], qkr[:, side, :]).then_inc(s_pc1, 1)

            def row_max(b, m):
                upto(dve, s_mxmm, b, 32, m + 1)
                dve.tensor_reduce(negmax[:, m // NT, m % NT:m % NT + 1], max_bank(m), AX.X, ALU.max,
                                  negate=True).then_inc(s_max, 1)

            def cut_max(b):
                nm = negmax[:].rearrange("p h j -> p j h")
                upto(dve, s_max, b, 32)
                upto(dve, s_mTmm, b - 1)
                dve.tensor_copy(mpc[:, :, 0, :], nm).then_inc(s_mp, 1)
                upto(dve, s_mp, b, 4, 1)
                dve.tensor_tensor(mres[:], nm, mpc[:, :, 0, :], ALU.subtract).then_inc(s_mp, 1)
                upto(dve, s_mp, b, 4, 2)
                dve.tensor_copy(mpc[:, :, 1, :], mres[:]).then_inc(s_mp, 1)
                upto(dve, s_mp, b, 4, 3)
                dve.tensor_tensor(mpc[:, :, 2, :], mres[:], mpc[:, :, 1, :], ALU.subtract).then_inc(s_mp, 1)

            def invert_den(b):
                upto(dve, s_denin, b, 16)
                upto(dve, s_rdout, b - 1, 16)
                dve.reciprocal(rden[:], den[:]).then_inc(s_rden, 1)

            def add_attention(b, u):
                upto(dve, s_projmm, b)
                upto(dve, s_hb, b)
                dve.tensor_tensor(h2[:, u], aux("project"), hb_sb[:, u], ALU.add).then_inc(s_h2, 1)

            def gate_first(b):
                upto(dve, s_gatmm, b)
                dve.tensor_copy(logit[:], aux("gates")[:, :, 0:NE + 1]).then_inc(s_logit, 1)
                upto(dve, s_logit, b)
                dve.tensor_reduce(lmax[:], logit[:, :, 0:NE], AX.X, ALU.max).then_inc(s_gate, 1)
                upto(dve, s_gate, b, 13, 1)
                dve.tensor_tensor(lsub[:, :, 0:NE], logit[:, :, 0:NE], lmax[:].unsqueeze(2).broadcast_to([P, NT, NE]),
                                  ALU.subtract).then_inc(s_gate, 1)
                dve.tensor_scalar(lsub[:, :, NE:NE + 1], logit[:, :, NE:NE + 1], -1.0, 87.0,
                                  ALU.mult, ALU.min).then_inc(s_gate, 1)

            def gate_second(b):
                upto(dve, s_gexp, b)
                dve.tensor_reduce(gden[:, :, 0:1], lexp[:, :, 0:NE], AX.X, ALU.add).then_inc(s_gate, 1)
                dve.tensor_scalar(gden[:, :, 1:2], lexp[:, :, NE:NE + 1], 1.0, None, ALU.add).then_inc(s_gate, 1)
                upto(dve, s_gate, b, 13, 5)
                dve.reciprocal(grec[:], gden[:]).then_inc(s_gate, 1)
                upto(dve, s_gate, b, 13, 6)
                dve.tensor_tensor(gsm[:], lexp[:, :, 0:NE], grec[:, :, 0:1].broadcast_to([P, NT, NE]),
                                  ALU.mult).then_inc(s_gate, 1)
                upto(dve, s_gate, b, 13, 7)
                dve.scalar_tensor_tensor(gad[:], grec[:, :, 1:2].broadcast_to([P, NT, NE]), -1.0 / NE, gsm[:],
                                         ALU.mult, ALU.add).then_inc(s_gate, 1)

            def gate_third(b):
                upto(dve, s_gate, b, 13, 8)
                dve.tensor_scalar(gsel[:], gad[:], 0.0, None, ALU.max).then_inc(s_gate, 1)
                upto(dve, s_gate, b, 13, 9)
                dve.tensor_reduce(wsum[:], gsel[:], AX.X, ALU.add).then_inc(s_gate, 1)
                upto(dve, s_gate, b, 13, 10)
                dve.scalar_tensor_tensor(wsafe[:], wsum[:], 0.0, wsum[:], ALU.is_equal, ALU.add).then_inc(s_gate, 1)
                upto(dve, s_gate, b, 13, 11)
                dve.reciprocal(wrec[:], wsafe[:]).then_inc(s_gate, 1)
                upto(dve, s_gate, b, 13, 12)
                upto(dve, s_wTmm, b - 1)
                dve.tensor_tensor(wts[:], gsel[:], wrec[:].unsqueeze(2).broadcast_to([P, NT, NE]),
                                  ALU.mult).then_inc(s_gate, 1)

            def weigh(b):
                upto(dve, s_lomm, b)
                upto(dve, s_win, b, 16)
                upto(dve, s_outmm, b - 1)
                dve.tensor_tensor(low[:], aux("low", 1), wrow[:], ALU.mult).then_inc(s_low, 1)

            def finish(b, u):
                upto(dve, s_outmm, b)
                upto(dve, s_store, b - 1, 16)
                dve.tensor_tensor(out_sb[:], aux("out"), h2[:, u], ALU.add).then_inc(s_out, 1)

            def tile_max(t, c, i):
                ahead = 2 if c >= MSTART else 1
                if runs(t + ahead):
                    row_max(t + ahead, 2 * ((c - MSTART) % SLOTS) + i)

            def step(t, u):
                old = (u - 2) % U
                for c in range(SLOTS):
                    if c == MSTART and runs(t + 1):
                        cut_max(t + 1)
                    tile_max(t, c, 0)
                    if c == 2 and runs(t - 2):
                        norm2(t - 2, old, (2, 3))
                    if c == 3 and runs(t + 2):
                        second(t + 2, 0)
                    if c == 6 and runs(t - 2):
                        gate_second(t - 2)
                    if c == 7 and runs(t - 1):
                        invert_den(t - 1)
                    if c == 8 and runs(t + 3):
                        stats(t + 3, h_sb, bn1, s_h, s_bn1)
                    if c == 15 and runs(t - 1):
                        stats(t - 1, h2[:, (u - 1) % U], bn2, s_h2, s_bn2)
                    tile_max(t, c, 1)
                    if c == 1 and runs(t - 2):
                        norm2(t - 2, old, (0, 1))
                    if c == 4 and runs(t + 2):
                        second(t + 2, 1)
                    if c == 4 and runs(t - 2):
                        gate_first(t - 2)
                    if c == 5 and runs(t + 3):
                        hot(t + 3)
                    if c == 6 and runs(t - 2):
                        gate_third(t - 2)
                    if c == 7 and runs(t + 3):
                        add_pos(t + 3)
                    if c == 8 and runs(t + 3):
                        moments(t + 3, bn1, mv1, s_bn1, s_mv1)
                    if c == 11 and runs(t - 2):
                        weigh(t - 2)
                    if c == 14 and runs(t - 1):
                        add_attention(t - 1, (u - 1) % U)
                    if c == 15 and runs(t - 1):
                        moments(t - 1, bn2, mv2, s_bn2, s_mv2)
                    if c == 15 and runs(t - 2):
                        finish(t - 2, old)

            steps(dve, step)


_INS = ["x", "posT", "catT", "consts", "ident", "tokW", "qkvT", "qkb", "bv", "ob", "woT", "wo_q", "gateT", "fc1T",
        "loA", "loBT", "fc2T"]


def kernel(**inputs):
    import numpy as np
    import concourse.bacc as bacc
    from concourse.bass_utils import run_bass_kernel_spmd

    a = {k.removeprefix("L0_"): np.asarray(v) for k, v in inputs.items()}
    f32 = np.float32

    nestT, segT = a["tok_nest_table"].T, a["tok_seg_table"].T
    catT = np.concatenate([nestT, nestT, nestT, np.zeros((P, SEGROW - 3 * NNEST), f32),
                           segT, segT, segT, np.zeros((P, HOT - SEGROW - 3 * NSEG), f32)], axis=1)
    qkv = a["attn_qkv_w"].reshape(NH, 3, HC, P)
    qkvb = a["attn_qkv_b"].reshape(NH, 3, HC)
    woT = a["attn_out_w"].T
    wo_q = woT.reshape(2, 4, HC, P).transpose(1, 0, 2, 3)
    gateT = np.zeros((P, NE + 1), f32)
    gateT[:, 0:NE] = a["ffn_gate_w"].T
    gateT[:, NE:NE + 1] = a["ffn_thr_w"].T
    loA = np.zeros((P, NE, Q), f32)
    loA[:, :, 0:NR] = a["ffn_lora_A"].transpose(1, 0, 2)
    loBT = np.zeros((P, NE, Q), f32)
    loBT[:, :, 0:NR] = a["ffn_lora_B"].transpose(2, 0, 1)

    consts = np.zeros((P, 4 + NH), f32)
    consts[:, 0] = -1
    for p in range(3):
        consts[p * NNEST:(p + 1) * NNEST, 0] = range(NNEST)
        consts[p * NNEST:(p + 1) * NNEST, 1 + p] = 1
        consts[SEGROW + p * NSEG:SEGROW + (p + 1) * NSEG, 0] = range(NSEG)
        consts[SEGROW + p * NSEG:SEGROW + (p + 1) * NSEG, 1 + p] = 1
        for h in range(NH):
            consts[STK + p * NH + h, 4 + h] = 1

    arrays = {
        "x": a["x"], "posT": a["tok_pos_table"].T, "catT": catT, "consts": consts, "ident": np.eye(P, dtype=f32),
        "tokW": a["tok_W"].reshape(3, P, P).transpose(1, 0, 2),
        "qkvT": qkv.transpose(3, 1, 0, 2).reshape(P, 3, P),
        "qkb": qkvb[:, 0:2].transpose(0, 2, 1).reshape(P, 2), "bv": qkvb[:, 2].reshape(P, 1),
        "ob": a["attn_out_b"].reshape(1, P), "woT": woT, "wo_q": wo_q.reshape(P, P), "gateT": gateT,
        "fc1T": a["ffn_fc1_w"].transpose(2, 0, 1), "loA": loA, "loBT": loBT,
        "fc2T": a["ffn_fc2_w"].transpose(2, 0, 1),
    }
    arrays = {f"in_{k}": np.ascontiguousarray(v) for k, v in arrays.items()}

    nc = bacc.Bacc("TRN2", target_bir_lowering=False, num_devices=1)
    args = [nc.dram_tensor(f"in_{k}", arrays[f"in_{k}"].shape, mybir.dt.from_np(arrays[f"in_{k}"].dtype),
                           kind="ExternalInput").ap() for k in _INS]
    args.append(nc.dram_tensor("out", (NSEQ, S, P), F32, kind="ExternalOutput").ap())
    tower(nc, *args)
    r = run_bass_kernel_spmd(nc, [arrays], core_ids=[0])
    return r.results[0]["out"]
```

```python
from contextlib import ExitStack

import concourse.bass as bass
from concourse import mybir

ALU = mybir.AluOpType
ACT = mybir.ActivationFunctionType
AX = mybir.AxisListType
F32 = mybir.dt.float32
BF16 = mybir.dt.bfloat16
I32 = mybir.dt.int32

P = 128
NSEQ, S = 32, 512
NT = S // P
NH, HC = 8, 16
NE, NR = 4, 16
Q = 32
NNEST, NSEG = 16, 8
SEGROW = 64
HOT = 96
STK = 6 * HC
KROWS = STK + 3 * NH
SLOTS = 16
TILES = NH * NT
MSTART = 10
RING, MIX = 3, 4
U = 4

PE_ORDER = [("max", 0), ("scores", 0), ("product", 0), ("scores", 1), ("max", 1), ("values", 0)]
PRODUCTS = [
    ("q", 2), ("k", 2), ("xn2T", -2), ("gates", -2), ("fc1_0", -2), ("fc1_1", -2), ("embed", 3), ("fc1_2", -2),
    ("fc1_3", -2), ("wT", -2), ("v", 2), ("mT", 1), ("low", -2), ("xnT", 3), ("project", -1), ("out", -2),
]
ACT_WORK = [
    (0, 1, "qk", 2, 0), (1, 1, "qk", 2, 1), (1, 2, "xn2T", -2, 0), (3, 2, "gate_exp", -2, 0), (4, 0, "ctx", -1, 1),
    (4, 1, "den_out", -1, 1), (4, 1, "relu", -2, 0), (6, 0, "relu", -2, 1), (6, 1, "relu", -2, 2),
    (8, 1, "relu", -2, 3), (9, 1, "wT", -2, 0), (9, 2, "weights_out", -2, 0), (10, 1, "v", 2, 0),
    (11, 1, "mT", 1, 0), (12, 1, "ctx", 0, 0), (13, 1, "max_in", 1, 0), (13, 2, "xnT", 3, 0),
    (14, 0, "den_out", 0, 0),
]
DVE_WORK = [
    (0, 2, "norm2", -2, 0), (1, 0, "norm2", -2, 1), (2, 1, "second", 2, 0), (3, 0, "second", 2, 1),
    (3, 1, "gate", -2, 0), (4, 0, "gate", -2, 1), (4, 2, "gate", -2, 2), (5, 2, "hot", 3, 0),
    (6, 1, "add_pos", 3, 0), (6, 2, "invert_den", -1, 0), (7, 1, "gate", -2, 3), (7, 2, "stats1", 3, 0),
    (9, 2, "moments1", 3, 0), (12, 1, "weigh", -2, 0), (14, 1, "add_attention", -1, 0), (15, 1, "stats2", -1, 0),
    (15, 2, "moments2", -1, 0), (15, 2, "finish", -2, 0),
]
POOL_WORK = [
    ("rstd1", 2, 0), ("norm", 2, 0), ("normalise", -2, 0), ("rstd2", -2, 0), ("residual", 2, 0), ("residual", 2, 1),
    ("third", 2, 0), ("third", 2, 1), ("add_bias", 2, 0),
]
SP_WORK = [
    ("ids", 3, 0), ("piece", 2, (0, 0)), ("piece", 2, (1, 0)), ("piece", 2, (0, 1)), ("piece", 2, (1, 1)),
    ("piece", 2, (0, 2)), ("piece", 2, (1, 2)), ("den_in", -1, 0), ("stack", 2, 0), ("stack", 2, 1),
    ("rden_out", -1, 0), ("rden_in", -1, 0), ("weights_in", -2, 0), ("out", -2, 0),
]

EPS = 1e-5
QSCALE = HC ** -0.5
Q_READS = [(0, 0, 3), (3 * HC, 0, 2), (5 * HC, 0, 1)]
K_READS = [(0, 0, 3), (3 * HC, 1, 2), (5 * HC, 2, 1)]


def tower(nc, x, posT, catT, consts, ident, tokW, qkvT, qkb, bv, ob, woT, wo_q, gateT, fc1T, loA, loBT, fc2T, out):
    ids_dram = nc.dram_tensor("ids_dram", (NSEQ, 2, S), BF16, kind="Internal").ap()
    stack_dram = nc.dram_tensor("stack_dram", (2, 3, HC, NH, S), BF16, kind="Internal").ap()
    den_dram = nc.dram_tensor("den_dram", (NH, S), F32, kind="Internal").ap()
    rden_dram = nc.dram_tensor("rden_dram", (2, 4, 2, S), F32, kind="Internal").ap()
    w_dram = nc.dram_tensor("w_dram", (NE, S), F32, kind="Internal").ap()

    with ExitStack() as ctx:
        def sb(name, shape, dt=F32):
            return ctx.enter_context(nc.sbuf_tensor(name, shape, dt))

        def sem(name):
            return ctx.enter_context(nc.semaphore(name))

        sc = ctx.enter_context(nc.psum_tensor("sc", [P, RING, S], F32))
        pv = ctx.enter_context(nc.psum_tensor("pv", [P, S], F32))
        mix = ctx.enter_context(nc.psum_tensor("mix", [P, MIX, S], F32))

        def aux(name, n=NT):
            bank = mix[:, (3 * [p for p, _ in PRODUCTS].index(name) + 1) % MIX]
            return bank if n == 1 else bank.rearrange("p (j n) -> p j n", j=n)

        def max_bank(m):
            return mix[:, (3 * ((MSTART + m // 2) % SLOTS) + 2 * (m % 2)) % MIX]

        probs = sb("probs", [P, 8, 2, S])
        posT_sb = probs[:, 6, 0, :]
        fc2T_sb = probs[:, 6, 1, :].rearrange("p (e n) -> p e n", e=NE)
        catT_sb = sb("catT_sb", [P, HOT])
        const_sb = sb("const_sb", [P, 4 + NH])
        id32 = sb("id32", [P, P])
        id16 = sb("id16", [P, P], BF16)
        tokW_sb = sb("tokW_sb", [P, 3, P])
        qkvT_sb = sb("qkvT_sb", [P, 3, P])
        qkb_sb = sb("qkb_sb", [P, 2])
        qb_sb = sb("qb_sb", [P, 1])
        bv_sb = sb("bv_sb", [P, 1])
        ob_sb = sb("ob_sb", [1, P])
        ones_sb = sb("ones_sb", [1, P])
        woT_sb = sb("woT_sb", [P, P])
        wo_q_sb = sb("wo_q_sb", [P, P])
        gateT_sb = sb("gateT_sb", [P, NE + 1])
        fc1T_sb = sb("fc1T_sb", [P, NE, P])
        loA_sb = sb("loA_sb", [P, NE, Q])
        loBT_sb = sb("loBT_sb", [P, NE, Q])
        exp_w = sb("exp_w", [P, P])
        posW = sb("posW", [P, NT, P])
        obias = sb("obias", [P, P])
        table = sb("table", [HOT, P], BF16)
        minus_half = sb("minus_half", [P, NT])
        eps_sb = sb("eps_sb", [P, NT])
        after = sb("after", [P, 1])

        xf, opens, closes, zeros, delta, depth, lowest = (probs[0:NSEQ, i // 2, i % 2, :] for i in range(7))
        xi, segi = (probs[0:NSEQ, 4, i, :].bitcast(I32) for i in range(2))
        ids_sb = sb("ids_sb", [NSEQ, 2, S], BF16)
        tab = probs[0:HOT, 7, 0, :].rearrange("p (i n) -> p i n", i=4)
        tab16 = sb("tab16", [HOT, 2, P], BF16)

        ids_b = sb("ids_b", [HOT, S], BF16)
        onehot = sb("onehot", [HOT, S], BF16)
        h_sb = sb("h_sb", [P, NT, P])
        hb_sb = sb("hb_sb", [P, U, NT, P])
        bn1 = sb("bn1", [P, NT, 6])
        mv1 = sb("mv1", [P, NT, 2])
        ve1 = sb("ve1", [P, NT])
        rstd1 = sb("rstd1", [P, NT])
        hc = sb("hc", [P, NT, P])
        xn = sb("xn", [P, NT, P])
        xnT = sb("xnT", [P, S])
        qk32 = sb("qk32", [P, 2, S])
        qkr = sb("qkr", [P, 2, S])
        pieces = sb("pieces", [P, 2, 3, S], BF16)
        vals = sb("vals", [P, U, NT, NH, Q])
        qstk = sb("qstk", [P, U, NH, S], BF16)
        kstk = sb("kstk", [P, U, NH, S], BF16)
        negmax = sb("negmax", [P, NH, NT])
        mres = sb("mres", [P, NT, NH])
        mpc = sb("mpc", [P, NT, 3, NH], BF16)
        mT = sb("mT", [3 * NH, S], BF16)
        ctx_sb = sb("ctx_sb", [P, 2, 2, S])
        den = sb("den", [P, Q])
        rden = sb("rden", [P, Q])
        rdenb = sb("rdenb", [P, 2, S])
        ctxh = sb("ctxh", [P, 2, S])
        ctxn = sb("ctxn", [P, S])
        h2 = sb("h2", [P, U, NT, P])
        bn2 = sb("bn2", [P, NT, 6])
        mv2 = sb("mv2", [P, NT, 2])
        ve2 = sb("ve2", [P, NT])
        rstd2 = sb("rstd2", [P, NT])
        xn2 = sb("xn2", [P, NT, P])
        xn2T = sb("xn2T", [P, S])
        logit = sb("logit", [P, NT, 5])
        lmax = sb("lmax", [P, NT])
        lsub = sb("lsub", [P, NT, 5])
        lexp = sb("lexp", [P, NT, 5])
        gden = sb("gden", [P, NT, 2])
        grec = sb("grec", [P, NT, 2])
        gsm = sb("gsm", [P, NT, NE])
        gad = sb("gad", [P, NT, NE])
        gsel = sb("gsel", [P, NT, NE])
        wsum = sb("wsum", [P, NT])
        wsafe = sb("wsafe", [P, NT])
        wrec = sb("wrec", [P, NT])
        wts = sb("wts", [P, NT, NE])
        wT = sb("wT", [NT * NE, P])
        wrow = sb("wrow", [P, S])
        hid = sb("hid", [P, NE, S])
        low = sb("low", [P, S])
        out_sb = sb("out_sb", [P, NT, P])

        s_x = sem("s_x")
        s_emb_w = sem("s_emb_w")
        s_w = sem("s_w")
        s_heads = sem("s_heads")
        s_set = sem("s_set")
        s_setmm = sem("s_setmm")
        s_setcp = sem("s_setcp")
        s_idset = sem("s_idset")
        s_qb = sem("s_qb")
        s_table = sem("s_table")
        s_idsout = sem("s_idsout")
        s_const = sem("s_const")
        s_pconst = sem("s_pconst")
        s_ids = sem("s_ids")
        s_hot = sem("s_hot")
        s_embmm, s_h, s_hb = sem("s_embmm"), sem("s_h"), sem("s_hb")
        s_bn1, s_mv1, s_ve1, s_rstd1, s_hc, s_xn = (sem(n) for n in ("s_bn1", "s_mv1", "s_ve1", "s_rstd1", "s_hc", "s_xn"))
        s_xnTmm, s_xnT = sem("s_xnTmm"), sem("s_xnT")
        s_qmm, s_kmm, s_vmm = sem("s_qmm"), sem("s_kmm"), sem("s_vmm")
        s_qk32 = sem("s_qk32")
        s_v = sem("s_v")
        s_pc0, s_res0, s_pc1, s_pc2 = sem("s_pc0"), sem("s_res0"), sem("s_pc1"), sem("s_pc2")
        s_pcout = [sem(f"s_pcout{a}") for a in "qk"]
        s_stk = [sem(f"s_stk{a}") for a in "qk"]
        s_mxmm, s_max = sem("s_mxmm"), sem("s_max")
        s_mp = sem("s_mp")
        s_mTmm, s_mT, s_mrow = sem("s_mTmm"), sem("s_mT"), sem("s_mrow")
        s_score, s_exp, s_pv, s_ctx = sem("s_score"), sem("s_exp"), sem("s_pv"), sem("s_ctx")
        s_denout, s_denin, s_rden, s_rdout = sem("s_denout"), sem("s_denin"), sem("s_rden"), sem("s_rdout")
        s_rdin = [sem(f"s_rdin{g}") for g in range(2)]
        s_ctxh, s_ctxn = sem("s_ctxh"), sem("s_ctxn")
        s_zrow = sem("s_zrow")
        s_projmm, s_h2 = sem("s_projmm"), sem("s_h2")
        s_bn2, s_mv2, s_ve2, s_rstd2, s_xn2 = sem("s_bn2"), sem("s_mv2"), sem("s_ve2"), sem("s_rstd2"), sem("s_xn2")
        s_xn2Tmm, s_xn2T = sem("s_xn2Tmm"), sem("s_xn2T")
        s_gatmm, s_logit = sem("s_gatmm"), sem("s_logit")
        s_gate = sem("s_gate")
        s_gexp = sem("s_gexp")
        s_wTmm, s_wT, s_wout, s_win = sem("s_wTmm"), sem("s_wT"), sem("s_wout"), sem("s_win")
        s_fc1mm, s_hid = sem("s_fc1mm"), sem("s_hid")
        s_lomm, s_low = sem("s_lomm"), sem("s_low")
        s_outmm, s_out, s_store = sem("s_outmm"), sem("s_out"), sem("s_store")

        def upto(eng, s, b, per=1, k=None):
            k = per if k is None else k
            if isinstance(b, int):
                value = min(per * b + k, per * NSEQ)
                if value > 0:
                    eng.wait_ge(s, value)
            else:
                eng.wait_ge(s, b * per + k)

        def ring_free(eng, s, b, i):
            upto(eng, s, b, TILES, i - RING + 1 if i >= RING else min(i - 1, 0))

        def runs(b):
            return not isinstance(b, int) or 0 <= b < NSEQ

        def steps(eng, step):
            first = 3
            rounds = (NSEQ - 3 - first) // U
            for t in range(-3, first):
                step(t, t % U)
            with eng.Fori(0, rounds) as i:
                for u in range(U):
                    step(i * U + (first + u), (first + u) % U)
            for t in range(first + rounds * U, NSEQ + 2):
                step(t, t % U)

        block = ctx.enter_context(nc.Block())

        @block.sync
        def _(sp):
            sp.dma_start(xi, x).then_inc(s_x, 16)
            for dst, src in [(posT_sb, posT), (tokW_sb[:], tokW), (catT_sb[:], catT), (const_sb[:], consts), (id32[:], ident)]:
                sp.dma_start(dst, src).then_inc(s_emb_w, 16)
            sp.wait_ge(s_idset, 2)
            sp.dma_start(ids_dram, ids_sb[:]).then_inc(s_idsout, 16)
            for g in range(2):
                sp.dma_start(rden_dram[g, :, 1 - g], zeros[0:4, :]).then_inc(s_zrow, 16)
            sp.wait_ge(s_idsout, 16)
            sp.wait_ge(s_zrow, 32)

            def load_ids(b):
                upto(sp, s_hot, b - 1)
                sp.dma_start(ids_b[0:SEGROW, :], ids_dram[b, 0].partition_broadcast(SEGROW)).then_inc(s_ids, 16)
                sp.dma_start(ids_b[SEGROW:HOT, :], ids_dram[b, 1].partition_broadcast(HOT - SEGROW)).then_inc(s_ids, 16)

            def store_piece(b, side, p):
                upto(sp, (s_pc0, s_pc1, s_pc2)[p], b, 2, side + 1)
                if p == 0:
                    upto(sp, s_stk[side], b - 1, 48)
                sp.dma_start(stack_dram[side, p].rearrange("c h s -> h c s"),
                             pieces[:, side, p, :]).then_inc(s_pcout[side], 16)

            def load_qstack(b, u):
                upto(sp, s_pcout[0], b, 48)
                upto(sp, s_score, b - U, TILES)
                for row, p, n in Q_READS:
                    sp.dma_start(qstk[row:row + n * HC, u, :, :],
                                 stack_dram[0, p:p + n].rearrange("p c h s -> (p c) h s")).then_inc(s_stk[0], 16)

            def load_kstack(b, u):
                upto(sp, s_pcout[1], b, 48)
                upto(sp, s_score, b - U, TILES)
                for row, p, n in K_READS:
                    sp.dma_start(kstk[row:row + n * HC, u, :, :],
                                 stack_dram[1, p].unsqueeze(0).broadcast_to([n, HC, NH, S])).then_inc(s_stk[1], 16)

            def load_den(b):
                upto(sp, s_denout, b, 32)
                upto(sp, s_rden, b - 1)
                sp.dma_start(den[:], den_dram.rearrange("h (k s) -> (h k) s", s=Q)).then_inc(s_denin, 16)

            def store_rden(b):
                for g in range(2):
                    upto(sp, s_rdin[g], b - 1, 16)
                upto(sp, s_rden, b)
                for g in range(2):
                    sp.dma_start(rden_dram[g, :, g].rearrange("q (k s) -> q k s", s=Q),
                                 rden[64 * g:64 * g + 64, :]).then_inc(s_rdout, 16)

            def load_rden(b):
                for g in range(2):
                    upto(sp, s_ctxh, b - 1, 2, g + 1)
                    if g == 0:
                        upto(sp, s_rdout, b, 32)
                    sp.dma_start(rdenb[:, g, :],
                                 rden_dram[g].rearrange("q a s -> (q a) s").unsqueeze(1).broadcast_to([8, HC, S])
                                 ).then_inc(s_rdin[g], 16)

            def load_weights(b):
                upto(sp, s_low, b - 1)
                upto(sp, s_wout, b, 16)
                sp.dma_start(wrow[:], w_dram.unsqueeze(1).broadcast_to([NE, Q, S])).then_inc(s_win, 16)

            def store_out(b):
                upto(sp, s_out, b)
                sp.dma_start(out[b].rearrange("(j p) d -> p j d", p=P), out_sb[:]).then_inc(s_store, 16)

            work = {
                "ids": lambda b, u, _: load_ids(b),
                "piece": lambda b, u, part: store_piece(b, *part),
                "stack": lambda b, u, side: (load_qstack, load_kstack)[side](b, u),
                "den_in": lambda b, u, _: load_den(b),
                "rden_out": lambda b, u, _: store_rden(b),
                "rden_in": lambda b, u, _: load_rden(b),
                "weights_in": lambda b, u, _: load_weights(b),
                "out": lambda b, u, _: store_out(b),
            }

            def step(t, u):
                for name, ahead, part in SP_WORK:
                    if runs(t + ahead):
                        work[name](t + ahead, (u + ahead) % U, part)

            nc.disable_value_cache = True
            steps(sp, step)
            nc.disable_value_cache = False
            sp.wait_ge(s_store, 16 * NSEQ)

        @block.gpsimd
        def _(pool):
            for v in range(U):
                pool.memset(vals[:, v, :, 0:4, HC:Q], 1.0).then_inc(s_pconst, 1)
                pool.memset(vals[:, v, :, 4:NH, 0:HC], 1.0).then_inc(s_pconst, 1)

            def rstd(b, mv, ve, rs, s_mv, s_ve, s_rs, s_used, n_used):
                upto(pool, s_mv, b, NT)
                upto(pool, s_used, b - 1, n_used)
                pool.tensor_tensor(ve[:], mv[:, :, 1], eps_sb[:], ALU.add).then_inc(s_ve, 1)
                upto(pool, s_ve, b)
                pool.tensor_tensor(rs[:], ve[:], minus_half[:], ALU.pow).then_inc(s_rs, 1)

            def add_bias(b, u):
                upto(pool, s_h, b)
                upto(pool, s_h2, b - U)
                pool.tensor_tensor(hb_sb[:, u], h_sb[:], obias[:].unsqueeze(1).broadcast_to([P, NT, P]),
                                   ALU.add).then_inc(s_hb, 1)

            def residual(b, side):
                upto(pool, s_pc0, b, 2, side + 1)
                pool.tensor_tensor(qkr[:, side, :], qk32[:, side, :], pieces[:, side, 0, :],
                                   ALU.subtract).then_inc(s_res0, 1)

            def third(b, side):
                upto(pool, s_pc1, b, 2, side + 1)
                upto(pool, s_pcout[side], b - 1, 48)
                pool.tensor_tensor(pieces[:, side, 2, :], qkr[:, side, :], pieces[:, side, 1, :],
                                   ALU.subtract).then_inc(s_pc2, 1)

            def norm(b):
                upto(pool, s_rstd1, b)
                pool.tensor_tensor(hc[:], h_sb[:], mv1[:, :, 0:1].broadcast_to([P, NT, P]),
                                   ALU.subtract).then_inc(s_hc, 1)
                upto(pool, s_hc, b)
                upto(pool, s_xnTmm, b - 1)
                pool.tensor_tensor(xn[:], hc[:], rstd1[:].unsqueeze(2).broadcast_to([P, NT, P]),
                                   ALU.mult).then_inc(s_xn, 1)

            def normalise(b, u):
                for g in range(2):
                    upto(pool, s_rdin[g], b, 16)
                    pool.tensor_tensor(ctxh[:, g, :], ctx_sb[:, u % 2, g, :], rdenb[:, g, :],
                                       ALU.mult).then_inc(s_ctxh, 1)
                upto(pool, s_ctxh, b, 2)
                upto(pool, s_projmm, b - 1)
                pool.tensor_tensor(ctxn[:], ctxh[:, 0, :], ctxh[:, 1, :], ALU.add).then_inc(s_ctxn, 1)

            pool.wait_ge(s_setcp, 4)
            pool.wait_ge(s_const, 3)

            work = {
                "rstd1": lambda b, u, _: rstd(b, mv1, ve1, rstd1, s_mv1, s_ve1, s_rstd1, s_xn, 1),
                "rstd2": lambda b, u, _: rstd(b, mv2, ve2, rstd2, s_mv2, s_ve2, s_rstd2, s_xn2, NT),
                "residual": lambda b, u, side: residual(b, side),
                "third": lambda b, u, side: third(b, side),
                "add_bias": lambda b, u, _: add_bias(b, u),
                "norm": lambda b, u, _: norm(b),
                "normalise": lambda b, u, _: normalise(b, u),
            }

            def step(t, u):
                for name, ahead, part in POOL_WORK:
                    if runs(t + ahead):
                        work[name](t + ahead, (u + ahead) % U, part)

            steps(pool, step)

        @block.scalar
        def _(act):
            weights = [(loBT_sb[:], loBT), (fc2T_sb, fc2T), (bv_sb[:], bv), (ob_sb[:], ob), (woT_sb[:], woT),
                       (qkb_sb[:], qkb), (qkvT_sb[:], qkvT), (wo_q_sb[:], wo_q), (gateT_sb[:], gateT),
                       (fc1T_sb[:], fc1T), (loA_sb[:], loA)]
            for dst, src in weights:
                act.dma_start(dst, src).then_inc(s_w, 16)
            act.wait_ge(s_w, 16 * len(weights))
            act.mul(qb_sb[:], qkb_sb[:, 0:1], QSCALE).then_inc(s_qb, 1)
            act.wait_ge(s_qb, 1)
            act.wait_ge(s_const, 4)
            for u in range(1, U):
                act.dma_start(kstk[STK:KROWS, u, :, :], kstk[STK:KROWS, 0, :, :]).then_inc(s_heads, 16)

            def exp(b, i):
                c = i // 2
                upto(act, s_score, b, TILES, i + 1)
                if i % 8 == 0:
                    upto(act, s_pv, b, 8, 2 * (c // 4) - 2)
                act.activation(probs[:, c % 8, i % 2], sc[:, i % RING], ACT.Exp).then_inc(s_exp, 1)

            def copy_xnT(b):
                upto(act, s_xnTmm, b)
                upto(act, s_vmm, b - 1)
                act.copy(xnT[:], aux("xnT", 1)).then_inc(s_xnT, 1)

            def copy_qk(b, side):
                upto(act, (s_qmm, s_kmm)[side], b)
                upto(act, s_res0, b - 1, 2, side + 1)
                act.activation(qk32[:, side, :], aux("qk"[side], 1), ACT.Identity,
                               bias=(qb_sb[:], qkb_sb[:, 1:2])[side], scale=(QSCALE, 1.0)[side]).then_inc(s_qk32, 1)
                upto(act, s_qk32, b, 2, side + 1)
                upto(act, s_pcout[side], b - 1, 48)
                act.copy(pieces[:, side, 0, :], qk32[:, side, :]).then_inc(s_pc0, 1)

            def copy_v(b, u):
                upto(act, s_vmm, b)
                upto(act, s_pv, b - U, 8)
                v = aux("v", 1).rearrange("p (j h c) -> p j h c", j=NT, h=NH)
                act.copy(vals[:, u, :, 0:4, 0:HC], v[:, :, 0:4]).then_inc(s_v, 1)
                act.copy(vals[:, u, :, 4:NH, HC:Q], v[:, :, 4:NH]).then_inc(s_v, 1)

            def copy_mT(b):
                upto(act, s_mTmm, b)
                upto(act, s_mrow, b - 1, 16)
                act.copy(mT[:], aux("mT", 1)[0:3 * NH]).then_inc(s_mT, 1)

            def store_den(b, g, u):
                upto(act, s_ctx, b, 2, g + 1)
                upto(act, s_denin, b - 1, 16)
                row = (HC, 0)[g]
                act.dma_start(den_dram[4 * g:4 * g + 4], ctx_sb[row:P:Q, u % 2, g, :]).then_inc(s_denout, 16)

            def store_weights(b):
                upto(act, s_wT, b)
                upto(act, s_win, b - 1, 16)
                act.dma_start(w_dram.rearrange("e (j n) -> j e n", n=P), wT[:]).then_inc(s_wout, 16)

            def load_max(b, u):
                upto(act, s_mT, b)
                act.dma_start(qstk[STK:KROWS, u, :, :],
                             mT[:].unsqueeze(1).broadcast_to([3 * NH, NH, S])).then_inc(s_mrow, 16)

            def copy_ctx(b, g, u):
                upto(act, s_pv, b, 8, 4 * g + 4)
                upto(act, s_ctxh, b - 2, 2, g + 1)
                upto(act, s_denout, b - 2, 32)
                act.copy(ctx_sb[:, u % 2, g, :], pv[:]).then_inc(s_ctx, 1)

            def copy_xn2T(b):
                upto(act, s_xn2Tmm, b)
                upto(act, s_fc1mm, b - 1, NE)
                act.copy(xn2T[:], aux("xn2T", 1)).then_inc(s_xn2T, 1)

            def gate_exp(b):
                upto(act, s_gate, b, 13, 3)
                upto(act, s_gate, b - 1, 13, 7)
                act.activation(lexp[:], lsub[:], ACT.Exp).then_inc(s_gexp, 1)

            def copy_wT(b):
                upto(act, s_wTmm, b)
                upto(act, s_wout, b - 1, 16)
                act.copy(wT[:], aux("wT", 1)[0:NT * NE, 0:P]).then_inc(s_wT, 1)

            def relu(b, e):
                upto(act, s_fc1mm, b, NE, e + 1)
                upto(act, s_lomm, b - 1)
                act.activation(hid[:, e, :], aux(f"fc1_{e}", 1), ACT.Relu).then_inc(s_hid, 1)

            work = {
                "qk": lambda b, u, side: copy_qk(b, side),
                "v": lambda b, u, _: copy_v(b, u),
                "xn2T": lambda b, u, _: copy_xn2T(b),
                "relu": lambda b, u, e: relu(b, e),
                "wT": lambda b, u, _: copy_wT(b),
                "mT": lambda b, u, _: copy_mT(b),
                "xnT": lambda b, u, _: copy_xnT(b),
                "ctx": lambda b, u, g: copy_ctx(b, g, u),
                "gate_exp": lambda b, u, _: gate_exp(b),
                "max_in": lambda b, u, _: load_max(b, u),
                "den_out": lambda b, u, g: store_den(b, g, u),
                "weights_out": lambda b, u, _: store_weights(b),
            }

            def step(t, u):
                for c in range(SLOTS):
                    for place in range(3):
                        for name, ahead, part in [w[2:] for w in ACT_WORK if w[:2] == (c, place)]:
                            if runs(t + ahead):
                                work[name](t + ahead, (u + ahead) % U, part)
                        if place < 2 and runs(t):
                            exp(t, 2 * c + place)

            steps(act, step)

        @block.tensor
        def _(pe):
            pe.wait_ge(s_emb_w, 16 * 5)

            for j in range(NT):
                mm = pe.matmul(mix[:, 0, j * P:(j + 1) * P], posT_sb[:, j * P:(j + 1) * P], tokW_sb[:, 0, :], start=True, stop=True)
            mm.then_inc(s_setmm, 1)
            pe.matmul(mix[0:SEGROW, 1, 0:P], catT_sb[:, 0:SEGROW], tokW_sb[:, 1, :], start=True, stop=True)
            pe.matmul(mix[SEGROW:HOT, 1, 0:P], catT_sb[:, SEGROW:HOT], tokW_sb[:, 2, :], start=True, stop=True).then_inc(s_setmm, 1)
            pe.wait_ge(s_w, 16 * 11)
            for e in range(NE):
                mm = pe.matmul(mix[Q * e:Q * e + Q, 2, 0:P], loBT_sb[:, e, :], fc2T_sb[:, e, :], start=True, stop=True)
            mm.then_inc(s_setmm, 1)
            pe.matmul(pv[:, 0:P], bv_sb[:].broadcast_to([P, P]), woT_sb[:], start=True, stop=False)
            pe.wait_ge(s_const, 1)
            pe.matmul(pv[:, 0:P], ones_sb[:], ob_sb[:], start=False, stop=True).then_inc(s_setmm, 1)
            pe.wait_ge(s_setcp, 4)
            pe.wait_ge(s_table, 1)
            pe.wait_ge(s_pconst, 2 * U)
            pe.wait_ge(s_const, 3)

            def scores_T(b, i, u):
                c, g = i // 2, i // 16
                half, h = c // 4 % 2, 4 * g + c % 4
                j = 2 * half + i % 2
                if i == 0:
                    upto(pe, s_mrow, b, 16)
                if i == 0 and isinstance(b, int) and b == 0:
                    pe.wait_ge(s_const, 4)
                    pe.wait_ge(s_heads, 16 * (U - 1))
                ring_free(pe, s_exp, b, i)
                pe.matmul(sc[:, i % RING, :], kstk[0:KROWS, u, h, j * P:(j + 1) * P],
                          qstk[0:KROWS, u, h, :], start=True, stop=True).then_inc(s_score, 1)

            def values(b, r, jj, u):
                g, half = r // 2, r % 2
                if jj == 0:
                    upto(pe, s_exp, b, TILES, 8 * r + 8)
                    if half == 0:
                        upto(pe, s_ctx, b, 2, g)
                for i in range(4):
                    mm = pe.matmul(pv[Q * i:Q * i + Q, :], vals[:, u, 2 * half + jj, 4 * g + i, :],
                                   probs[:, 4 * (r % 2) + i, jj, :],
                                   start=(half == 0 and jj == 0), stop=(half == 1 and jj == 1))
                mm.then_inc(s_pv, 1)

            def scores(b, m, u):
                h, j = m // NT, m % NT
                if m == 0:
                    for side in range(2):
                        upto(pe, s_stk[side], b, 48)
                pe.matmul(max_bank(m), qstk[0:STK, u, h, j * P:(j + 1) * P],
                          kstk[0:STK, u, h, :], start=True, stop=True).then_inc(s_mxmm, 1)

            def embed(b):
                upto(pe, s_hot, b)
                for j in range(NT):
                    mm = pe.matmul(aux("embed")[:, j, :], onehot[:, j * P:(j + 1) * P], table[:], start=True, stop=True)
                mm.then_inc(s_embmm, 1)

            def turn(b, name, src, ready, n_ready, signal):
                upto(pe, ready, b, n_ready)
                for j in range(NT):
                    mm = pe.transpose(aux(name)[:, j, :], src[:, j, :], id32[:])
                mm.then_inc(signal, 1)

            def qk(b, side):
                upto(pe, s_xnT, b)
                pe.matmul(aux("qk"[side], 1), qkvT_sb[:, side, :], xnT[:], start=True, stop=True).then_inc((s_qmm, s_kmm)[side], 1)

            def v(b):
                upto(pe, s_xnT, b)
                for j in range(NT):
                    mm = pe.matmul(aux("v")[:, j, :], xnT[:, j * P:(j + 1) * P], qkvT_sb[:, 2, :], start=True, stop=True)
                mm.then_inc(s_vmm, 1)

            def turn_max(b):
                upto(pe, s_mp, b, 4)
                for j in range(NT):
                    mm = pe.matmul(aux("mT")[0:3 * NH, j, :], mpc[:, j].rearrange("p a h -> p (a h)"), id16[:],
                                   start=True, stop=True)
                mm.then_inc(s_mTmm, 1)

            def project(b):
                upto(pe, s_ctxn, b)
                for j in range(NT):
                    mm = pe.matmul(aux("project")[:, j, :], ctxn[:, j * P:(j + 1) * P], wo_q_sb[:], start=True, stop=True)
                mm.then_inc(s_projmm, 1)

            def gates(b):
                upto(pe, s_xn2T, b)
                for j in range(NT):
                    mm = pe.matmul(aux("gates")[:, j, 0:NE + 1], xn2T[:, j * P:(j + 1) * P], gateT_sb[:],
                                   start=True, stop=True)
                mm.then_inc(s_gatmm, 1)

            def fc1(b, e):
                upto(pe, s_xn2T, b)
                pe.matmul(aux(f"fc1_{e}", 1), fc1T_sb[:, e, :], xn2T[:], start=True, stop=True).then_inc(s_fc1mm, 1)

            def low_rank(b):
                upto(pe, s_hid, b, NE)
                for e in range(NE):
                    mm = pe.matmul(aux("low", 1)[Q * e:Q * e + Q], loA_sb[:, e, :], hid[:, e, :], start=True, stop=True)
                mm.then_inc(s_lomm, 1)

            def turn_weights(b):
                upto(pe, s_gate, b, 13)
                pe.transpose(aux("wT", 1)[0:NT * NE, 0:P], wts[:].rearrange("p j e -> p (j e)"), id32[:]).then_inc(s_wTmm, 1)

            def experts_out(b):
                upto(pe, s_low, b)
                for j in range(NT):
                    mm = pe.matmul(aux("out")[:, j, :], low[:, j * P:(j + 1) * P], exp_w[:], start=True, stop=True)
                mm.then_inc(s_outmm, 1)

            products = {
                "q": (lambda b: qk(b, 0), (s_qk32, 2, 1)),
                "k": (lambda b: qk(b, 1), (s_qk32, 2, 2)),
                "v": (v, (s_v, 2, 2)),
                "xn2T": (lambda b: turn(b, "xn2T", xn2, s_xn2, NT, s_xn2Tmm), (s_xn2T, 1, 1)),
                "gates": (gates, (s_logit, 1, 1)),
                "fc1_0": (lambda b: fc1(b, 0), (s_hid, NE, 1)),
                "fc1_1": (lambda b: fc1(b, 1), (s_hid, NE, 2)),
                "wT": (turn_weights, (s_wT, 1, 1)),
                "fc1_2": (lambda b: fc1(b, 2), (s_hid, NE, 3)),
                "fc1_3": (lambda b: fc1(b, 3), (s_hid, NE, 4)),
                "embed": (embed, (s_h, 1, 1)),
                "low": (low_rank, (s_low, 1, 1)),
                "mT": (turn_max, (s_mT, 1, 1)),
                "xnT": (lambda b: turn(b, "xnT", xn, s_xn, 1, s_xnTmm), (s_xnT, 1, 1)),
                "project": (project, (s_h2, 1, 1)),
                "out": (experts_out, (s_out, 1, 1)),
            }

            def mix_user(t, n):
                t, c, kind = t + n // (3 * SLOTS), n // 3 % SLOTS, n % 3
                if kind == 1:
                    name, ahead = PRODUCTS[c]
                    return t + ahead, products[name][1]
                return t + (2 if c >= MSTART else 1), (s_max, TILES, 2 * ((c - MSTART) % SLOTS) + kind // 2 + 1)

            def mix_free(t, n):
                for before in range(n - MIX, -6 * SLOTS, -MIX):
                    b, (read, per, k) = mix_user(t, before)
                    if runs(b):
                        upto(pe, read, b, per, k)
                        return

            def row_tile(t, u, c, i):
                ahead = 2 if c >= MSTART else 1
                if runs(t + ahead):
                    mix_free(t, 3 * c + 2 * i)
                    scores(t + ahead, 2 * ((c - MSTART) % SLOTS) + i, (u + ahead) % U)

            def product(t, c):
                name, ahead = PRODUCTS[c]
                if runs(t + ahead):
                    mix_free(t, 3 * c + 1)
                    products[name][0](t + ahead)

            def step(t, u):
                for c in range(SLOTS):
                    for what, i in PE_ORDER:
                        if what == "scores" and runs(t):
                            scores_T(t, 2 * c + i, u)
                        if what == "max":
                            row_tile(t, u, c, i)
                        if what == "product":
                            product(t, c)
                        if what == "values" and c % 2 == 1:
                            r, jj = c // 4 - 1, c // 2 % 2
                            if r >= 0 and runs(t):
                                values(t, r, jj, u)
                            if r < 0 and runs(t - 1):
                                values(t - 1, 3, jj, (u - 1) % U)

            nc.disable_value_cache = True
            steps(pe, step)
            nc.disable_value_cache = False

        @block.vector
        def _(dve):
            n_set = [0]

            def link(ins):
                n_set[0] += 1
                ins.then_inc(s_set, 1)
                dve.wait_ge(s_set, n_set[0])

            link(dve.memset(zeros, 0.0))
            dve.memset(ones_sb[:], 1.0).then_inc(s_const, 1)
            dve.wait_ge(s_x, 16)
            link(dve.tensor_copy(xf, xi))
            link(dve.tensor_scalar(opens, xf, 40.0, None, ALU.is_equal))
            link(dve.scalar_tensor_tensor(opens, xf, 123.0, opens, ALU.is_equal, ALU.add))
            link(dve.scalar_tensor_tensor(opens, xf, 91.0, opens, ALU.is_equal, ALU.add))
            link(dve.tensor_scalar(closes, xf, 41.0, None, ALU.is_equal))
            link(dve.scalar_tensor_tensor(closes, xf, 125.0, closes, ALU.is_equal, ALU.add))
            link(dve.scalar_tensor_tensor(closes, xf, 93.0, closes, ALU.is_equal, ALU.add))
            link(dve.tensor_tensor(delta, opens, closes, ALU.subtract))
            link(dve.tensor_tensor_scan(depth, delta, zeros, 0.0, ALU.add, ALU.add))
            link(dve.tensor_tensor_scan(lowest, depth, zeros, 0.0, ALU.min, ALU.min))
            link(dve.tensor_tensor(depth, depth, lowest, ALU.subtract))
            dve.tensor_scalar(ids_sb[:, 0, :], depth, 0.0, float(NNEST - 1), ALU.max, ALU.min).then_inc(s_idset, 1)
            link(dve.tensor_scalar(xf, xf, 39990.0, None, ALU.is_gt))
            link(dve.tensor_tensor_scan(segi, xf, zeros, 0.0, ALU.add, ALU.add))
            link(dve.tensor_scalar(segi, segi, NSEG - 1, None, ALU.bitwise_and))
            dve.tensor_copy(ids_sb[:, 1, :], segi).then_inc(s_idset, 1)

            dve.wait_ge(s_emb_w, 16 * 5)
            dve.tensor_copy(id16[:], id32[:]).then_inc(s_const, 1)
            dve.memset(eps_sb[:], EPS)
            dve.memset(minus_half[:], -0.5).then_inc(s_const, 1)

            dve.wait_ge(s_setmm, 1)
            dve.tensor_copy(posW[:], mix[:, 0].rearrange("p (j n) -> p j n", j=NT)).then_inc(s_setcp, 1)
            dve.wait_ge(s_setmm, 2)
            dve.tensor_copy(tab[:, 0, :], mix[0:HOT, 1, 0:P]).then_inc(s_setcp, 1)
            dve.wait_ge(s_setmm, 3)
            dve.tensor_copy(exp_w[:], mix[:, 2, 0:P]).then_inc(s_setcp, 1)
            dve.wait_ge(s_setmm, 4)
            dve.tensor_copy(obias[:], pv[:, 0:P]).then_inc(s_setcp, 1)

            dve.wait_ge(s_setcp, 2)
            link(dve.tensor_copy(tab16[:, 0, :], tab[:, 0, :]))
            link(dve.tensor_tensor(tab[:, 1, :], tab[:, 0, :], tab16[:, 0, :], ALU.subtract))
            link(dve.tensor_copy(tab16[:, 1, :], tab[:, 1, :]))
            link(dve.tensor_tensor(tab[:, 2, :], tab[:, 1, :], tab16[:, 1, :], ALU.subtract))
            link(dve.tensor_scalar(tab[:, 3, :], tab16[:, 0, :], const_sb[0:HOT, 1:2], None, ALU.mult))
            link(dve.scalar_tensor_tensor(tab[:, 0, :], tab16[:, 1, :], const_sb[0:HOT, 2:3], tab[:, 3, :],
                                          ALU.mult, ALU.add))
            dve.scalar_tensor_tensor(table[:], tab[:, 2, :], const_sb[0:HOT, 3:4], tab[:, 0, :],
                                     ALU.mult, ALU.add).then_inc(s_table, 1)

            dve.tensor_copy(kstk[STK:KROWS, 0, :, :],
                            const_sb[STK:KROWS, 4:4 + NH].unsqueeze(2).broadcast_to([3 * NH, NH, S])).then_inc(s_const, 1)

            def hot(b):
                upto(dve, s_ids, b, 32)
                upto(dve, s_embmm, b - 1)
                dve.tensor_scalar(onehot[:], ids_b[:], const_sb[0:HOT, 0:1], None, ALU.is_equal).then_inc(s_hot, 1)

            def add_pos(b):
                upto(dve, s_embmm, b)
                upto(dve, s_hb, b - 1)
                upto(dve, s_hc, b - 1)
                dve.tensor_tensor(h_sb[:], aux("embed"), posW[:], ALU.add).then_inc(s_h, 1)

            def stats(b, src, bn, s_src, s_bn):
                upto(dve, s_src, b)
                for j in range(NT):
                    dve.bn_stats(bn[:, j, :], src[:, j, :]).then_inc(s_bn, 1)

            def moments(b, bn, mv, s_bn, s_mv):
                upto(dve, s_bn, b, NT)
                dve.memset(after[:], 0.0)
                for j in range(NT):
                    dve.bn_aggr(mv[:, j, :], bn[:, j, :]).then_inc(s_mv, 1)

            def norm2(b, u, tiles):
                upto(dve, s_rstd2, b)
                upto(dve, s_xn2Tmm, b - 1)
                for j in tiles:
                    dve.tensor_scalar(xn2[:, j, :], h2[:, u, j, :], mv2[:, j, 0:1], rstd2[:, j:j + 1],
                                      ALU.subtract, ALU.mult).then_inc(s_xn2, 1)

            def second(b, side):
                upto(dve, s_res0, b, 2, side + 1)
                upto(dve, s_pcout[side], b - 1, 48)
                dve.tensor_copy(pieces[:, side, 1, :], qkr[:, side, :]).then_inc(s_pc1, 1)

            def row_max(b, m):
                upto(dve, s_mxmm, b, 32, m + 1)
                dve.tensor_reduce(negmax[:, m // NT, m % NT:m % NT + 1], max_bank(m), AX.X, ALU.max,
                                  negate=True).then_inc(s_max, 1)

            def cut_max(b):
                nm = negmax[:].rearrange("p h j -> p j h")
                upto(dve, s_max, b, 32)
                upto(dve, s_mTmm, b - 1)
                dve.tensor_copy(mpc[:, :, 0, :], nm).then_inc(s_mp, 1)
                upto(dve, s_mp, b, 4, 1)
                dve.tensor_tensor(mres[:], nm, mpc[:, :, 0, :], ALU.subtract).then_inc(s_mp, 1)
                upto(dve, s_mp, b, 4, 2)
                dve.tensor_copy(mpc[:, :, 1, :], mres[:]).then_inc(s_mp, 1)
                upto(dve, s_mp, b, 4, 3)
                dve.tensor_tensor(mpc[:, :, 2, :], mres[:], mpc[:, :, 1, :], ALU.subtract).then_inc(s_mp, 1)

            def invert_den(b):
                upto(dve, s_denin, b, 16)
                upto(dve, s_rdout, b - 1, 16)
                dve.reciprocal(rden[:], den[:]).then_inc(s_rden, 1)

            def add_attention(b, u):
                upto(dve, s_projmm, b)
                upto(dve, s_hb, b)
                dve.tensor_tensor(h2[:, u], aux("project"), hb_sb[:, u], ALU.add).then_inc(s_h2, 1)

            def gate_first(b):
                upto(dve, s_gatmm, b)
                dve.tensor_copy(logit[:], aux("gates")[:, :, 0:NE + 1]).then_inc(s_logit, 1)
                upto(dve, s_logit, b)
                dve.tensor_reduce(lmax[:], logit[:, :, 0:NE], AX.X, ALU.max).then_inc(s_gate, 1)
                upto(dve, s_gate, b, 13, 1)
                dve.tensor_tensor(lsub[:, :, 0:NE], logit[:, :, 0:NE], lmax[:].unsqueeze(2).broadcast_to([P, NT, NE]),
                                  ALU.subtract).then_inc(s_gate, 1)
                dve.tensor_scalar(lsub[:, :, NE:NE + 1], logit[:, :, NE:NE + 1], -1.0, 87.0,
                                  ALU.mult, ALU.min).then_inc(s_gate, 1)

            def gate_second(b):
                upto(dve, s_gexp, b)
                dve.tensor_reduce(gden[:, :, 0:1], lexp[:, :, 0:NE], AX.X, ALU.add).then_inc(s_gate, 1)
                dve.tensor_scalar(gden[:, :, 1:2], lexp[:, :, NE:NE + 1], 1.0, None, ALU.add).then_inc(s_gate, 1)
                upto(dve, s_gate, b, 13, 5)
                dve.reciprocal(grec[:], gden[:]).then_inc(s_gate, 1)
                upto(dve, s_gate, b, 13, 6)
                dve.tensor_tensor(gsm[:], lexp[:, :, 0:NE], grec[:, :, 0:1].broadcast_to([P, NT, NE]),
                                  ALU.mult).then_inc(s_gate, 1)
                upto(dve, s_gate, b, 13, 7)
                dve.scalar_tensor_tensor(gad[:], grec[:, :, 1:2].broadcast_to([P, NT, NE]), -1.0 / NE, gsm[:],
                                         ALU.mult, ALU.add).then_inc(s_gate, 1)

            def gate_third(b):
                upto(dve, s_gate, b, 13, 8)
                dve.tensor_scalar(gsel[:], gad[:], 0.0, None, ALU.max).then_inc(s_gate, 1)
                upto(dve, s_gate, b, 13, 9)
                dve.tensor_reduce(wsum[:], gsel[:], AX.X, ALU.add).then_inc(s_gate, 1)

            def gate_fourth(b):
                upto(dve, s_gate, b, 13, 10)
                dve.scalar_tensor_tensor(wsafe[:], wsum[:], 0.0, wsum[:], ALU.is_equal, ALU.add).then_inc(s_gate, 1)
                upto(dve, s_gate, b, 13, 11)
                dve.reciprocal(wrec[:], wsafe[:]).then_inc(s_gate, 1)
                upto(dve, s_gate, b, 13, 12)
                upto(dve, s_wTmm, b - 1)
                dve.tensor_tensor(wts[:], gsel[:], wrec[:].unsqueeze(2).broadcast_to([P, NT, NE]),
                                  ALU.mult).then_inc(s_gate, 1)

            def weigh(b):
                upto(dve, s_lomm, b)
                upto(dve, s_win, b, 16)
                upto(dve, s_outmm, b - 1)
                dve.tensor_tensor(low[:], aux("low", 1), wrow[:], ALU.mult).then_inc(s_low, 1)

            def finish(b, u):
                upto(dve, s_outmm, b)
                upto(dve, s_store, b - 1, 16)
                dve.tensor_tensor(out_sb[:], aux("out"), h2[:, u], ALU.add).then_inc(s_out, 1)

            def tile_max(t, c, i):
                ahead = 2 if c >= MSTART else 1
                if runs(t + ahead):
                    row_max(t + ahead, 2 * ((c - MSTART) % SLOTS) + i)

            work = {
                "hot": lambda b, u, _: hot(b),
                "add_pos": lambda b, u, _: add_pos(b),
                "stats1": lambda b, u, _: stats(b, h_sb, bn1, s_h, s_bn1),
                "moments1": lambda b, u, _: moments(b, bn1, mv1, s_bn1, s_mv1),
                "second": lambda b, u, side: second(b, side),
                "invert_den": lambda b, u, _: invert_den(b),
                "add_attention": lambda b, u, _: add_attention(b, u),
                "stats2": lambda b, u, _: stats(b, h2[:, u], bn2, s_h2, s_bn2),
                "moments2": lambda b, u, _: moments(b, bn2, mv2, s_bn2, s_mv2),
                "norm2": lambda b, u, half: norm2(b, u, (2 * half, 2 * half + 1)),
                "gate": lambda b, u, part: (gate_first, gate_second, gate_third, gate_fourth)[part](b),
                "weigh": lambda b, u, _: weigh(b),
                "finish": lambda b, u, _: finish(b, u),
            }

            def step(t, u):
                for c in range(SLOTS):
                    if c == MSTART and runs(t + 1):
                        cut_max(t + 1)
                    for place in range(3):
                        for name, ahead, part in [w[2:] for w in DVE_WORK if w[:2] == (c, place)]:
                            if runs(t + ahead):
                                work[name](t + ahead, (u + ahead) % U, part)
                        if place < 2:
                            tile_max(t, c, place)

            steps(dve, step)


_INS = ["x", "posT", "catT", "consts", "ident", "tokW", "qkvT", "qkb", "bv", "ob", "woT", "wo_q", "gateT", "fc1T",
        "loA", "loBT", "fc2T"]


def kernel(**inputs):
    import numpy as np
    import concourse.bacc as bacc
    from concourse.bass_utils import run_bass_kernel_spmd

    a = {k.removeprefix("L0_"): np.asarray(v) for k, v in inputs.items()}
    f32 = np.float32

    nestT, segT = a["tok_nest_table"].T, a["tok_seg_table"].T
    catT = np.concatenate([nestT, nestT, nestT, np.zeros((P, SEGROW - 3 * NNEST), f32),
                           segT, segT, segT, np.zeros((P, HOT - SEGROW - 3 * NSEG), f32)], axis=1)
    qkv = a["attn_qkv_w"].reshape(NH, 3, HC, P)
    qkvb = a["attn_qkv_b"].reshape(NH, 3, HC)
    woT = a["attn_out_w"].T
    wo_q = woT.reshape(2, 4, HC, P).transpose(1, 0, 2, 3)
    gateT = np.zeros((P, NE + 1), f32)
    gateT[:, 0:NE] = a["ffn_gate_w"].T
    gateT[:, NE:NE + 1] = a["ffn_thr_w"].T
    loA = np.zeros((P, NE, Q), f32)
    loA[:, :, 0:NR] = a["ffn_lora_A"].transpose(1, 0, 2)
    loBT = np.zeros((P, NE, Q), f32)
    loBT[:, :, 0:NR] = a["ffn_lora_B"].transpose(2, 0, 1)

    consts = np.zeros((P, 4 + NH), f32)
    consts[:, 0] = -1
    for p in range(3):
        consts[p * NNEST:(p + 1) * NNEST, 0] = range(NNEST)
        consts[p * NNEST:(p + 1) * NNEST, 1 + p] = 1
        consts[SEGROW + p * NSEG:SEGROW + (p + 1) * NSEG, 0] = range(NSEG)
        consts[SEGROW + p * NSEG:SEGROW + (p + 1) * NSEG, 1 + p] = 1
        for h in range(NH):
            consts[STK + p * NH + h, 4 + h] = 1

    arrays = {
        "x": a["x"], "posT": a["tok_pos_table"].T, "catT": catT, "consts": consts, "ident": np.eye(P, dtype=f32),
        "tokW": a["tok_W"].reshape(3, P, P).transpose(1, 0, 2),
        "qkvT": qkv.transpose(3, 1, 0, 2).reshape(P, 3, P),
        "qkb": qkvb[:, 0:2].transpose(0, 2, 1).reshape(P, 2), "bv": qkvb[:, 2].reshape(P, 1),
        "ob": a["attn_out_b"].reshape(1, P), "woT": woT, "wo_q": wo_q.reshape(P, P), "gateT": gateT,
        "fc1T": a["ffn_fc1_w"].transpose(2, 0, 1), "loA": loA, "loBT": loBT,
        "fc2T": a["ffn_fc2_w"].transpose(2, 0, 1),
    }
    arrays = {f"in_{k}": np.ascontiguousarray(v) for k, v in arrays.items()}

    nc = bacc.Bacc("TRN2", target_bir_lowering=False, num_devices=1)
    args = [nc.dram_tensor(f"in_{k}", arrays[f"in_{k}"].shape, mybir.dt.from_np(arrays[f"in_{k}"].dtype),
                           kind="ExternalInput").ap() for k in _INS]
    args.append(nc.dram_tensor("out", (NSEQ, S, P), F32, kind="ExternalOutput").ap())
    tower(nc, *args)
    r = run_bass_kernel_spmd(nc, [arrays], core_ids=[0])
    return r.results[0]["out"]
```
